# Optimizing a Trainium2 kernel written in Bass

```python
import numpy as np
import jax
import jax.numpy as jnp

def _softmax(x, axis=-1):
    return jax.nn.softmax(x, axis=axis)

def _gelu(x):
    return jax.nn.gelu(x, approximate=True)

def _silu(x):
    return jax.nn.silu(x)

def _sigmoid(x):
    return jax.nn.sigmoid(x)

def _layernorm(x, axis=-1, eps=1e-05):
    m = jnp.mean(x, axis=axis, keepdims=True)
    v = jnp.var(x, axis=axis, keepdims=True)
    return (x - m) / jnp.sqrt(v + eps)

def _scatter_add(tgt, idx, src, axis=0):
    return tgt.at[idx].add(src)

def _segment_sum(src, seg, n):
    return jax.ops.segment_sum(src, seg, n)
kernel_name = 'mk_recurrent_d2_jaxref_r4_23b6a4'

def setup_inputs(seed: int=0):
    np.random.seed(seed)
    _w = jnp.asarray

    def _L0_attn_setup():
        import jax, jax.numpy as jnp
        import numpy as np
        D = 256
        H = 16
        KVH = 4
        HD = D // H
        LAT = 64
        WIN = 64
        B, S = (1, 512)
        BASE_G, BASE_L = (1000000.0, 10000.0)
        EPS = 1e-06

        def rmsnorm(x, w):
            return x * jax.lax.rsqrt(jnp.mean(x * x, axis=-1, keepdims=True) + EPS) * w

        def qk_norm(x):
            return x * jax.lax.rsqrt(jnp.mean(x * x, axis=-1, keepdims=True) + EPS)

        def rope(x, base):
            s, hd = (x.shape[-2], x.shape[-1])
            inv_freq = 1.0 / base ** (jnp.arange(0, hd, 2, dtype=jnp.float32) / hd)
            freqs = jnp.arange(s, dtype=jnp.float32)[:, None] * inv_freq[None, :]
            cos, sin = (jnp.cos(freqs), jnp.sin(freqs))
            xe, xo = (x[..., ::2], x[..., 1::2])
            out = jnp.stack([xe * cos - xo * sin, xe * sin + xo * cos], axis=-1)
            return out.reshape(x.shape)

        def split_heads(x, n_heads):
            b, s, _ = x.shape
            return x.reshape(b, s, n_heads, HD).transpose(0, 2, 1, 3)

        def repeat_kv(x):
            return jnp.repeat(x, H // KVH, axis=1)

        def sdpa(q, k, v, mask):
            scores = jnp.einsum('bhqd,bhkd->bhqk', q, k) / np.sqrt(HD).astype(np.float32)
            scores = jnp.where(mask, scores, jnp.float32(-1e+30))
            probs = jax.nn.softmax(scores, axis=-1)
            return jnp.einsum('bhqk,bhkd->bhqd', probs, v)

        def merge_heads(x):
            b, h, s, hd = x.shape
            return x.transpose(0, 2, 1, 3).reshape(b, s, h * hd)

        def global_latent_attn(x, wq, w_kv_down, w_k_up, w_v_up, wo):
            q = split_heads(x @ wq, H)
            latent = x @ w_kv_down
            k = split_heads(latent @ w_k_up, KVH)
            v = split_heads(latent @ w_v_up, KVH)
            q, k = (rope(q, BASE_G), rope(k, BASE_G))
            q, k = (qk_norm(q), qk_norm(k))
            k, v = (repeat_kv(k), repeat_kv(v))
            i = jnp.arange(x.shape[1])
            causal = i[:, None] >= i[None, :]
            return merge_heads(sdpa(q, k, v, causal)) @ wo

        def local_gqa_attn(x, wq, wk, wv, wo):
            q = split_heads(x @ wq, H)
            k = split_heads(x @ wk, KVH)
            v = split_heads(x @ wv, KVH)
            q, k = (rope(q, BASE_L), rope(k, BASE_L))
            q, k = (qk_norm(q), qk_norm(k))
            k, v = (repeat_kv(k), repeat_kv(v))
            i = jnp.arange(x.shape[1])
            diff = i[:, None] - i[None, :]
            mask = (diff >= 0) & (diff < WIN)
            return merge_heads(sdpa(q, k, v, mask)) @ wo
        key = jax.random.key(seed)
        ks = jax.random.split(key, 12)
        std = 0.02
        return {'hidden': jax.random.normal(ks[0], (B, S, D), dtype=jnp.float32), 'norm1_w': jnp.ones((D,), jnp.float32), 'norm2_w': jnp.ones((D,), jnp.float32), 'g_wq': jax.random.normal(ks[1], (D, H * HD), jnp.float32) * std, 'g_kv_down': jax.random.normal(ks[2], (D, LAT), jnp.float32) * std, 'g_k_up': jax.random.normal(ks[3], (LAT, KVH * HD), jnp.float32) * std, 'g_v_up': jax.random.normal(ks[4], (LAT, KVH * HD), jnp.float32) * std, 'g_wo': jax.random.normal(ks[5], (D, D), jnp.float32) * std, 'l_wq': jax.random.normal(ks[6], (D, H * HD), jnp.float32) * std, 'l_wk': jax.random.normal(ks[7], (D, KVH * HD), jnp.float32) * std, 'l_wv': jax.random.normal(ks[8], (D, KVH * HD), jnp.float32) * std, 'l_wo': jax.random.normal(ks[9], (D, D), jnp.float32) * std}
    _L0_attn_in = _L0_attn_setup()

    def _L0_ffn_setup():
        import jax, jax.numpy as jnp
        import numpy as np
        IN_FEATURES = 256
        ACT_BITS = 4

        def _hadamard(size: int) -> np.ndarray:
            h = np.array([[1.0]], dtype=np.float64)
            while h.shape[0] < size:
                h = np.block([[h, h], [h, -h]])
            return (h / np.sqrt(size)).astype(np.float32)

        def _quantize_activations(x, bits=ACT_BITS):
            pos = 2 ** (bits - 1) - 1
            neg = 2 ** (bits - 1)
            scale = jnp.clip(jnp.max(jnp.abs(jax.lax.stop_gradient(x)), axis=-1, keepdims=True), 1e-05) / pos
            q = jnp.clip(jnp.round(x / scale), -neg, pos) * scale
            return x + jax.lax.stop_gradient(q - x)

        def _ternary_quantize_ste(w):
            scale = jnp.clip(jnp.mean(jnp.abs(jax.lax.stop_gradient(w)), axis=1, keepdims=True), 1e-05)
            n = w / scale
            tern = jnp.where(n > 0.5, 1.0, jnp.where(n < -0.5, -1.0, 0.0))
            q = tern * scale
            return w + jax.lax.stop_gradient(q - w)
        key = jax.random.key(seed)
        k1, k2 = jax.random.split(key)
        x = jax.random.normal(k1, (8, 2048, IN_FEATURES), dtype=jnp.float32)
        bound = 1.0 / np.sqrt(IN_FEATURES)
        weight = jax.random.uniform(k2, (256, IN_FEATURES), dtype=jnp.float32, minval=-bound, maxval=bound)
        return {'x': x, 'weight': weight}
    _L0_ffn_in = _L0_ffn_setup()

    def _L1_attn_setup():
        import jax, jax.numpy as jnp
        import numpy as np
        BATCH, SEQ, DMODEL, DHID = (4, 1024, 256, 256)
        R_MIN, R_MAX = (0.9, 0.99)
        MAX_PHASE = np.pi / 50
        EPS = 1e-05
        key = jax.random.key(seed)
        ks = jax.random.split(key, 8)
        u1 = jax.random.uniform(ks[0], (DHID,)) * (1 - EPS) + EPS
        mag_sq = u1 * (R_MAX ** 2 - R_MIN ** 2) + R_MIN ** 2
        nu_log = jnp.log(-0.5 * jnp.log(mag_sq + EPS))
        u2 = jax.random.uniform(ks[1], (DHID,)) * (1 - EPS) + EPS
        theta_log = jnp.log(MAX_PHASE * u2)
        B_re = jax.random.normal(ks[2], (DHID, DMODEL)) / np.sqrt(2 * DMODEL)
        B_im = jax.random.normal(ks[3], (DHID, DMODEL)) / np.sqrt(2 * DMODEL)
        C_re = jax.random.normal(ks[4], (DMODEL, DHID)) / np.sqrt(DHID)
        C_im = jax.random.normal(ks[5], (DMODEL, DHID)) / np.sqrt(DHID)
        D_skip = jax.random.normal(ks[6], (DMODEL,))
        inputs = jax.random.normal(ks[7], (BATCH, SEQ, DMODEL), dtype=jnp.float32)
        return {'inputs': inputs, 'nu_log': nu_log, 'theta_log': theta_log, 'B_re': B_re, 'B_im': B_im, 'C_re': C_re, 'C_im': C_im, 'D_skip': D_skip}
    _L1_attn_in = _L1_attn_setup()

    def _L1_ffn_setup():
        import jax, jax.numpy as jnp
        import numpy as np
        N_EXPERTS = 8
        CAP_FACTOR = 1.25
        BATCH, SEQ, DMODEL, DFF = (4, 512, 256, 1024)
        key = jax.random.key(seed)
        k0, k1, k2, k3 = jax.random.split(key, 4)
        x = jax.random.normal(k0, (BATCH, SEQ, DMODEL), dtype=jnp.float32)
        Wr = jax.random.normal(k1, (DMODEL, N_EXPERTS), dtype=jnp.float32) * 0.02
        W1 = jax.random.normal(k2, (N_EXPERTS, DMODEL, DFF), dtype=jnp.float32) * 0.02
        W2 = jax.random.normal(k3, (N_EXPERTS, DFF, DMODEL), dtype=jnp.float32) * 0.02
        return {'x': x, 'Wr': Wr, 'W1': W1, 'W2': W2}
    _L1_ffn_in = _L1_ffn_setup()
    _d = {'L0_attn_hidden': _L0_attn_in['hidden'], 'L0_attn_norm1_w': _L0_attn_in['norm1_w'], 'L0_attn_norm2_w': _L0_attn_in['norm2_w'], 'L0_attn_g_wq': _L0_attn_in['g_wq'], 'L0_attn_g_kv_down': _L0_attn_in['g_kv_down'], 'L0_attn_g_k_up': _L0_attn_in['g_k_up'], 'L0_attn_g_v_up': _L0_attn_in['g_v_up'], 'L0_attn_g_wo': _L0_attn_in['g_wo'], 'L0_attn_l_wq': _L0_attn_in['l_wq'], 'L0_attn_l_wk': _L0_attn_in['l_wk'], 'L0_attn_l_wv': _L0_attn_in['l_wv'], 'L0_attn_l_wo': _L0_attn_in['l_wo'], 'L0_ffn_weight': _L0_ffn_in['weight'], 'L1_attn_nu_log': _L1_attn_in['nu_log'], 'L1_attn_theta_log': _L1_attn_in['theta_log'], 'L1_attn_B_re': _L1_attn_in['B_re'], 'L1_attn_B_im': _L1_attn_in['B_im'], 'L1_attn_C_re': _L1_attn_in['C_re'], 'L1_attn_C_im': _L1_attn_in['C_im'], 'L1_attn_D_skip': _L1_attn_in['D_skip'], 'L1_ffn_Wr': _L1_ffn_in['Wr'], 'L1_ffn_W1': _L1_ffn_in['W1'], 'L1_ffn_W2': _L1_ffn_in['W2']}
    _x0 = _d['L0_attn_hidden']
    _d['L0_attn_hidden'] = jax.random.normal(jax.random.fold_in(jax.random.key(seed), 1), (32, 512, 256), dtype=_x0.dtype)
    del _x0
    return _d

def reference(L0_attn_hidden, L0_attn_norm1_w, L0_attn_norm2_w, L0_attn_g_wq, L0_attn_g_kv_down, L0_attn_g_k_up, L0_attn_g_v_up, L0_attn_g_wo, L0_attn_l_wq, L0_attn_l_wk, L0_attn_l_wv, L0_attn_l_wo, L0_ffn_weight, L1_attn_nu_log, L1_attn_theta_log, L1_attn_B_re, L1_attn_B_im, L1_attn_C_re, L1_attn_C_im, L1_attn_D_skip, L1_ffn_Wr, L1_ffn_W1, L1_ffn_W2):

    def _L0_attn_ref(hidden, norm1_w, norm2_w, g_wq, g_kv_down, g_k_up, g_v_up, g_wo, l_wq, l_wk, l_wv, l_wo):
        import jax, jax.numpy as jnp
        import numpy as np
        D = 256
        H = 16
        KVH = 4
        HD = D // H
        LAT = 64
        WIN = 64
        B, S = (1, 512)
        BASE_G, BASE_L = (1000000.0, 10000.0)
        EPS = 1e-06

        def rmsnorm(x, w):
            return x * jax.lax.rsqrt(jnp.mean(x * x, axis=-1, keepdims=True) + EPS) * w

        def qk_norm(x):
            return x * jax.lax.rsqrt(jnp.mean(x * x, axis=-1, keepdims=True) + EPS)

        def rope(x, base):
            s, hd = (x.shape[-2], x.shape[-1])
            inv_freq = 1.0 / base ** (jnp.arange(0, hd, 2, dtype=jnp.float32) / hd)
            freqs = jnp.arange(s, dtype=jnp.float32)[:, None] * inv_freq[None, :]
            cos, sin = (jnp.cos(freqs), jnp.sin(freqs))
            xe, xo = (x[..., ::2], x[..., 1::2])
            out = jnp.stack([xe * cos - xo * sin, xe * sin + xo * cos], axis=-1)
            return out.reshape(x.shape)

        def split_heads(x, n_heads):
            b, s, _ = x.shape
            return x.reshape(b, s, n_heads, HD).transpose(0, 2, 1, 3)

        def repeat_kv(x):
            return jnp.repeat(x, H // KVH, axis=1)

        def sdpa(q, k, v, mask):
            scores = jnp.einsum('bhqd,bhkd->bhqk', q, k) / np.sqrt(HD).astype(np.float32)
            scores = jnp.where(mask, scores, jnp.float32(-1e+30))
            probs = jax.nn.softmax(scores, axis=-1)
            return jnp.einsum('bhqk,bhkd->bhqd', probs, v)

        def merge_heads(x):
            b, h, s, hd = x.shape
            return x.transpose(0, 2, 1, 3).reshape(b, s, h * hd)

        def global_latent_attn(x, wq, w_kv_down, w_k_up, w_v_up, wo):
            q = split_heads(x @ wq, H)
            latent = x @ w_kv_down
            k = split_heads(latent @ w_k_up, KVH)
            v = split_heads(latent @ w_v_up, KVH)
            q, k = (rope(q, BASE_G), rope(k, BASE_G))
            q, k = (qk_norm(q), qk_norm(k))
            k, v = (repeat_kv(k), repeat_kv(v))
            i = jnp.arange(x.shape[1])
            causal = i[:, None] >= i[None, :]
            return merge_heads(sdpa(q, k, v, causal)) @ wo

        def local_gqa_attn(x, wq, wk, wv, wo):
            q = split_heads(x @ wq, H)
            k = split_heads(x @ wk, KVH)
            v = split_heads(x @ wv, KVH)
            q, k = (rope(q, BASE_L), rope(k, BASE_L))
            q, k = (qk_norm(q), qk_norm(k))
            k, v = (repeat_kv(k), repeat_kv(v))
            i = jnp.arange(x.shape[1])
            diff = i[:, None] - i[None, :]
            mask = (diff >= 0) & (diff < WIN)
            return merge_heads(sdpa(q, k, v, mask)) @ wo
        x = hidden
        x = x + global_latent_attn(rmsnorm(x, norm1_w), g_wq, g_kv_down, g_k_up, g_v_up, g_wo)
        x = x + local_gqa_attn(rmsnorm(x, norm2_w), l_wq, l_wk, l_wv, l_wo)
        return x

    def _L0_ffn_ref(x, weight):
        import jax, jax.numpy as jnp
        import numpy as np
        IN_FEATURES = 256
        ACT_BITS = 4

        def _hadamard(size: int) -> np.ndarray:
            h = np.array([[1.0]], dtype=np.float64)
            while h.shape[0] < size:
                h = np.block([[h, h], [h, -h]])
            return (h / np.sqrt(size)).astype(np.float32)

        def _quantize_activations(x, bits=ACT_BITS):
            pos = 2 ** (bits - 1) - 1
            neg = 2 ** (bits - 1)
            scale = jnp.clip(jnp.max(jnp.abs(jax.lax.stop_gradient(x)), axis=-1, keepdims=True), 1e-05) / pos
            q = jnp.clip(jnp.round(x / scale), -neg, pos) * scale
            return x + jax.lax.stop_gradient(q - x)

        def _ternary_quantize_ste(w):
            scale = jnp.clip(jnp.mean(jnp.abs(jax.lax.stop_gradient(w)), axis=1, keepdims=True), 1e-05)
            n = w / scale
            tern = jnp.where(n > 0.5, 1.0, jnp.where(n < -0.5, -1.0, 0.0))
            q = tern * scale
            return w + jax.lax.stop_gradient(q - w)
        H = jnp.asarray(_hadamard(IN_FEATURES))
        xh = x @ H
        xq = _quantize_activations(xh)
        wq = _ternary_quantize_ste(weight)
        return jnp.einsum('bsi,oi->bso', xq, wq)

    def _L1_attn_ref(inputs, nu_log, theta_log, B_re, B_im, C_re, C_im, D_skip):
        import jax, jax.numpy as jnp
        import numpy as np
        BATCH, SEQ, DMODEL, DHID = (4, 1024, 256, 256)
        R_MIN, R_MAX = (0.9, 0.99)
        MAX_PHASE = np.pi / 50
        EPS = 1e-05
        nu = jnp.exp(nu_log)
        theta = jnp.exp(theta_log)
        diag_lambda = jnp.exp(-nu + 1j * theta)
        gamma_log = 0.5 * jnp.log(1 - jnp.exp(-2 * jnp.exp(nu_log)) + EPS)
        B_norm = (B_re + 1j * B_im) * jnp.exp(gamma_log)[:, None]
        inputs_c = inputs.astype(jnp.complex64)
        Bu = jnp.einsum('hd,btd->bth', B_norm, inputs_c)

        def step(h, bu_t):
            h = diag_lambda * h + bu_t
            return (h, h)
        h0 = jnp.zeros((inputs.shape[0], diag_lambda.shape[0]), dtype=Bu.dtype)
        _, hs = jax.lax.scan(step, h0, jnp.swapaxes(Bu, 0, 1))
        hs = jnp.swapaxes(hs, 0, 1)
        C_complex = C_re + 1j * C_im
        out = jnp.einsum('bth,dh->btd', hs, C_complex).real + inputs * D_skip
        return out.astype(jnp.float32)

    def _L1_ffn_ref(x, Wr, W1, W2):
        import jax, jax.numpy as jnp
        import numpy as np
        N_EXPERTS = 8
        CAP_FACTOR = 1.25
        BATCH, SEQ, DMODEL, DFF = (4, 512, 256, 1024)
        B, S, D = x.shape
        E = W1.shape[0]
        cap = int(CAP_FACTOR * B * S / E)
        t = x.reshape(-1, D)
        probs = jax.nn.softmax(t @ Wr, axis=-1)
        idx = jnp.argmax(probs, axis=-1)
        pmax = jnp.max(probs, axis=-1)
        onehot = jax.nn.one_hot(idx, E, dtype=jnp.int32)
        pos = jnp.sum(jnp.cumsum(onehot, axis=0) * onehot, axis=-1) - 1
        kept = pos < cap
        flat = idx * cap + jnp.minimum(pos, cap - 1)
        disp = jnp.zeros((E * cap, D), t.dtype).at[flat].add(t * kept[:, None].astype(t.dtype))
        ein = disp.reshape(E, cap, D)
        h = jax.nn.relu(jnp.einsum('ecd,edf->ecf', ein, W1))
        eout = jnp.einsum('ecf,efd->ecd', h, W2).reshape(E * cap, D)
        comb = jnp.where(kept[:, None], eout[flat], t)
        factor = jnp.where(kept, pmax, jnp.ones_like(pmax))
        out = (comb * factor[:, None]).reshape(B, S, D)
        return out
    x = L0_attn_hidden
    xn = _layernorm(x, axis=-1)
    s = _L0_attn_ref(xn, L0_attn_norm1_w, L0_attn_norm2_w, L0_attn_g_wq, L0_attn_g_kv_down, L0_attn_g_k_up, L0_attn_g_v_up, L0_attn_g_wo, L0_attn_l_wq, L0_attn_l_wk, L0_attn_l_wv, L0_attn_l_wo)
    g = _silu(_L0_ffn_ref(xn, L0_ffn_weight))
    x = x + s * g
    xn = _layernorm(x, axis=-1)
    s = _L1_attn_ref(xn, L1_attn_nu_log, L1_attn_theta_log, L1_attn_B_re, L1_attn_B_im, L1_attn_C_re, L1_attn_C_im, L1_attn_D_skip)
    g = _silu(_L1_ffn_ref(xn, L1_ffn_Wr, L1_ffn_W1, L1_ffn_W2))
    x = x + s * g
    return x

_drawn_inputs = setup_inputs


def setup_inputs(seed=0):
    import zlib

    import numpy as np

    out = dict(_drawn_inputs(seed))
    spreads = {'L0_attn_norm1_w': (1.0, 0.6), 'L0_attn_norm2_w': (1.0, 0.6)}
    factors = {'L0_attn_g_wq': 8.0,
     'L0_attn_g_kv_down': 8.0,
     'L0_attn_g_k_up': 8.0,
     'L0_attn_g_v_up': 8.0,
     'L0_attn_g_wo': 8.0,
     'L0_attn_l_wq': 8.0,
     'L0_attn_l_wk': 8.0,
     'L0_attn_l_wv': 8.0,
     'L0_attn_l_wo': 8.0,
     'L1_attn_nu_log': 8.0,
     'L1_attn_theta_log': 64.0,
     'L1_attn_B_re': 6.117,
     'L1_attn_B_im': 6.127,
     'L1_attn_C_re': 6.133,
     'L1_attn_C_im': 6.145,
     'L1_attn_D_skip': 4.163,
     'L1_ffn_Wr': 3.213,
     'L1_ffn_W1': 3.58,
     'L1_ffn_W2': 2.981}
    for name, (base, spread) in spreads.items():
        noise = np.random.default_rng([zlib.crc32(name.encode()), seed]).standard_normal(out[name].shape)
        drawn = base * np.exp(spread * noise) if base else spread * noise
        out[name] = jnp.asarray(drawn.astype(out[name].dtype))
    for name, factor in factors.items():
        out[name] = (out[name] * factor).astype(out[name].dtype)
    return out
```

```python
from contextlib import ExitStack

import numpy as np

import concourse.bass as bass
from concourse import mybir

F32 = mybir.dt.float32
F16 = mybir.dt.float16
BF16 = mybir.dt.bfloat16
U32 = mybir.dt.uint32
ALU = mybir.AluOpType
ACT = mybir.ActivationFunctionType
AX = mybir.AxisListType

P = 128
NSEQ, S, D = 32, 512, 256
T = S // P
KT = D // P
H, KVH, HD = 16, 4, 16
GH = H // KVH
NQK = (H + KVH) * HD
NQKV = NQK + KVH * HD
LAT = 64
WIN = 64
E = 8
DFF = 1024
FT = DFF // P
NTOK = NSEQ * S
CAP = int(1.25 * NTOK / E)
NSLOT = E * CAP
SLOTS = 512
STEPS = CAP // SLOTS
MAGIC = 12582912.0
TWO_PI = 2.0 * np.pi
assert CAP % SLOTS == 0 and KT == 2 and T == 4


def width(kind, kb):
    rest = S - P * kb
    return rest if kind == 0 else min(rest, P + WIN)


def chunks(kind, kb):
    n = min(GH, 512 // width(kind, kb))
    return [(h, n) for h in range(0, GH, n)]


NCHUNK = [sum(len(chunks(k, kb)) for kb in range(T)) * KVH for k in range(2)]
STEPS_A = KVH * T
LAG = 3
STEP_ORDER = [(g, kb) for g in range(KVH) for kb in range(T)]
STEP = 2
LOCAL_AT = STEP * STEPS_A
FRONT, GATE, GLOBAL, BETWEEN, LOCAL, ENDING, BACK = 2, 1, 1, 0, 0, -1, -1


def came(s, lag=1):
    return not isinstance(s, int) or s >= lag


class Signal:

    def __init__(self, sem, per):
        self.sem, self.per = sem, per

    def at(self, s, k=None):
        return s * self.per + (self.per if k is None else k)

    def before(self, s, k=0, lag=1):
        return (s - lag + 1) * self.per + k

    def was(self, s, k=0, lag=1):
        return not isinstance(s, int) or self.before(s, k, lag) > 0


def runs(t, offset):
    return not isinstance(t, int) or 0 <= t + offset < NSEQ


def turns_done(t, offset):
    return min(max(t + offset, 0), NSEQ) if isinstance(t, int) else t + offset


class Attending:

    def __init__(self, sem, per):
        self.sem, self.per = sem, per

    def at(self, s, kind, k):
        t = s - (LOCAL if kind else GLOBAL)
        n = turns_done(t, GLOBAL) * self.per[0] + turns_done(t, LOCAL) * self.per[1] + k
        return n + self.per[0] if kind and runs(t, GLOBAL) else n

    def was(self, s, kind, k):
        return not isinstance(s, int) or self.at(s, kind, k) > 0


class Pair:

    def __init__(self, sems, per):
        self.sems, self.per = sems, 16 * per

    def at(self, s, b):
        return (s - b) * (self.per // 2) + self.per

    def total(self, n):
        return n // 2 * self.per


class Chain:

    def __init__(self, sem):
        self.sem, self.per, self.n, self.s = sem, 0, 0, 0

    def start(self, s):
        if came(s):
            self.per = self.per or self.n
        self.s, self.n = s, 0

    def inc(self, ins):
        ins.then_inc(self.sem, 1)
        self.n += 1

    def at(self):
        return self.s * self.per + self.n


PLAN = [
    (ENDING, {"a1_0": 9, "a1_1": 9, "o1_0": 11, "o1_1": 14}),
    (GLOBAL, {"a0_0": 41, "a0_1": 41, "o0_0": 43, "o0_1": 45}),
    (BETWEEN, {"yT0": 0, "yT1": 0, "p1_0": 3, "p1_1": 4, "p1_2": 6, "p1_3": 7, "k1_0": 22, "k1_1": 23,
               "q1_0": 24, "q1_1": 25, "q1_2": 27, "q1_3": 28}),
    (GATE, {"ffn0": 10, "ffn1": 12}),
    (BACK, {"zT0": 21, "zT1": 21, "logit": 23, "count": 27, "u0_0": 27, "u0_1": 27, "u1_0": 37, "u1_1": 37,
            "out0": 50, "out1": 52}),
    (FRONT, {"xT0": 16, "xT1": 16, "p0_0": 20, "p0_1": 22, "p0_2": 24, "p0_3": 29, "had0": 31, "had1": 33,
             "k0_0": 42, "k0_1": 43, "q0_0": 44, "q0_1": 46, "q0_2": 48, "q0_3": 49, "qT": 39}),
]
TICK = {n: t for _, names in PLAN for n, t in names.items()}
TAKEN = {"had0": 36, "had1": 36}
SIDE = [use[2:] for use in sorted((t, rank, n, off) for rank, (off, names) in enumerate(PLAN) for n, t in names.items())]

SUMS = [(f"{c}{kind}_{g}", off) for kind, off in ((0, GLOBAL), (1, LOCAL))
        for c, g in (("O", 0), ("O", 1), ("r", 0), ("O", 2), ("r", 1), ("O", 3), ("r", 2), ("r", 3))]
BANK_OF = {n: (0, 1, 4)[i % 3] for i, (n, _) in enumerate(SIDE)} | {n: 2 + int(n[-1]) % 2 for n, _ in SUMS}
BANK_USES = [[(n, off) for n, off in SIDE + SUMS if BANK_OF[n] == b] for b in range(5)]
OFFSET_OF = dict(SIDE + SUMS)


def shape_constants():
    i = np.arange(P)
    had = np.array([[1.0]])
    while had.shape[0] < D:
        had = np.block([[had, had], [had, -had]])
    had = (had / np.sqrt(D)).astype(np.float32)
    ropes = []
    for base in (1000000.0, 10000.0):
        inv = (np.float32(1.0) / np.float32(base) ** (np.arange(0, HD, 2, dtype=np.float32) / np.float32(HD))).astype(np.float32)
        ang = (np.arange(S, dtype=np.float32)[:, None] * inv[None, :]).astype(np.float32)
        for f in (np.cos, np.sin):
            ropes.append(f(ang.astype(np.float64)).astype(np.float32).reshape(T, P, HD // 2).transpose(1, 0, 2))
    rope = np.stack(ropes, axis=1).reshape(P, 4 * T * HD // 2)
    small = np.concatenate([np.tile(np.arange(E), (P, 1)), np.tile(E - np.arange(E), (P, 1)),
                            NSLOT + i[:, None] + P * np.arange(T)[None, :]], axis=1)
    return {
        "c_ident": np.eye(P, dtype=np.float32),
        "c_had": had,
        "c_upto": (i[:, None] <= i[None, :]).astype(np.float32),
        "c_rope": np.ascontiguousarray(rope.astype(np.float32)),
        "c_small": np.ascontiguousarray(small.astype(np.float32)),
        "c_time": np.tile(np.arange(S, dtype=np.float32), (P, 1)),
    }


def build_program(nc, a, out):
    ctx = ExitStack()
    with ctx:
        def sb(name, shape, dt=F32):
            return ctx.enter_context(nc.sbuf_tensor(name, [P] + shape, dt))

        def sem(name):
            return ctx.enter_context(nc.semaphore(name))

        def signal(name, per):
            return Signal(sem(name), per)

        def pair(name, per):
            return Pair([sem(f"{name}{b}") for b in range(2)], per)

        slots = nc.dram_tensor("slots", [NSLOT + NTOK, D], F32, kind="Internal").ap()
        kept_x = nc.dram_tensor("kept_x", [NTOK, D], F32, kind="Internal").ap()
        kept_s = nc.dram_tensor("kept_s", [NTOK, D], F32, kind="Internal").ap()
        kept_idx = nc.dram_tensor("kept_idx", [NSEQ * P, T], U32, kind="Internal").ap()
        kept_fac = nc.dram_tensor("kept_fac", [NSEQ * P, T], F32, kind="Internal").ap()

        def rows(dram, s):
            return dram[bass.ds(s * S, S), :].rearrange("(t p) d -> p t d", p=P)

        def slot_rows(n):
            return slots[bass.ds(n * SLOTS, SLOTS), :].rearrange("(t p) d -> p t d", p=P)

        def w1_rows(e):
            return a["W1"].rearrange("e d f -> (e d) f")[bass.ds(e * D, D), :].rearrange("(k p) f -> p k f", p=P)

        def w2_rows(e):
            return a["W2"].rearrange("e f d -> (e f) d")[bass.ds(e * DFF, DFF), :].rearrange("(k p) d -> p k d", p=P)

        ident = sb("ident", [P])
        ident_bf = sb("ident_bf", [P], BF16)
        ident_h = sb("ident_h", [P], F16)
        had = sb("had", [KT, D])
        upto_bf = sb("upto_bf", [P], BF16)
        ones_bf = sb("ones_bf", [P], BF16)
        rope = sb("rope", [2, 2, T, HD // 2])
        small = sb("small", [2 * E + T])
        eps = sb("eps", [4])
        normw = sb("normw", [2, KT])
        wqkv = [sb(f"wqkv{k}", [KT, NQKV]) for k in range(2)]
        wo = [sb(f"wo{k}", [KT, D]) for k in range(2)]
        ternT = sb("ternT", [KT, D], BF16)
        tern_scale = sb("tern_scale", [D])
        wr = sb("wr", [KT, E])
        bT = [sb(f"bT{c}", [KT, D]) for c in range(2)]
        cT = [sb(f"cT{c}", [KT, D]) for c in range(2)]
        dskip = sb("dskip", [D])
        lru_raw = sb("lru_raw", [2, KT])
        cosT = sb("cosT", [KT, S])
        sinT = sb("sinT", [KT, S])
        lam = sb("lam", [KT])

        x_in = sb("x_in", [T, D])
        zeros = sb("zeros", [D])
        xn = [sb(f"xn{b}", [T, D]) for b in range(2)]
        x2 = [sb(f"x2{b}", [T, D]) for b in range(2)]
        xT = sb("xT", [KT, S])
        qk = sb("qk", [T, NQK])
        rot = sb("rot", [T, NQK])
        tmp = [sb(f"tmp{k}", [T, D]) for k in range(3)]
        ropetmp = [sb(f"ropetmp{k}", [T, NQK // 2]) for k in range(4)]
        v_sb = [sb(f"v_sb{k}", [T, KVH, 32]) for k in range(3)]
        qx = sb("qx", [T, H, 64], F16)
        kx = sb("kx", [T, KVH, 2, 64], F16)
        qT = [sb(f"qT{k}", [H // 2, S], F16) for k in range(2)]
        kT = [sb(f"kT{k}", [2, T, KVH, P], F16) for k in range(2)]
        probs_all = sb("probs_all", [sum(GH * width(0, kb) for kb in range(T))])
        probs_at = np.cumsum([0] + [GH * width(0, kb) for kb in range(T)]).tolist()
        oT = [sb(f"oT{b}", [S]) for b in range(2)]
        attn = sb("attn", [T, D])
        attnT = sb("attnT", [KT, S])
        downT, ups, upto, ones = attn[:, 0, :], attn[:, 1, 0:2 * KVH * HD], attn[:, 2, 0:P], attn[:, 3, 0:P]
        gate = [sb(f"gate{b}", [T, D]) for b in range(2)]
        zT = sb("zT", [KT, S])
        q_int = sb("q_int", [T, D], BF16)
        rounded = xT[:, :, :].rearrange("p k t -> p (k t)").rearrange("p (t d) -> p t d", t=T)
        q_intT = sb("q_intT", [KT, S], BF16)
        x1 = sb("x1", [T, D])
        xn2 = sb("xn2", [T, D])
        s_out = sb("s_out", [T, D])
        lru = [tmp[k // 2][:, k % 2 * 2:k % 2 * 2 + 2, :].rearrange("p t d -> p (t d)") for k in range(6)]
        first_half = [sb(f"first_half{c}", [S]) for c in range(2)]
        hid = [[first_half[0], lru[0]], [first_half[1], lru[2]]]
        stats = [sb(f"stats{k}", [T, 6]) for k in range(2)]
        mv = [sb(f"mv{k}", [T, 2]) for k in range(2)]
        sc = sb("sc", [24, T])
        (RSTD, M1, M2, R1, LN, RSTD2, SS2, R2, AMAX, QSC, QINV, MX, MX2, SE, PM, POS, EID, KEPT,
         FLAT, DIFF, NK, LN2, LN3) = range(23)
        nrm = sb("nrm", [3, T * (H + KVH)])
        rden = [sb(f"rden{b}", [T, GH]) for b in range(2)]
        lg = sb("lg", [5, T, E])
        oh_bf = sb("oh_bf", [T, E], BF16)
        base = sb("base", [E])
        tokid = sb("tokid", [T])
        idx = [sb(f"idx{b}", [T], U32) for b in range(2)]
        fac = [sb(f"fac{b}", [T]) for b in range(2)]

        w1 = [q[:, :, :].rearrange("p h s -> p (h s)").bitcast(F32).rearrange("p (k f) -> p k f", k=KT) for q in qT]
        w2 = [k[:, :, :, :, :].rearrange("p b t g k -> p (b t g k)").bitcast(F32).rearrange("p (f d) -> p f d", f=FT)
              for k in kT]
        rows_in, rows_out = [x_in, x2[0]], [x1, attn]
        rowsT = [xT, zT]
        end_x1, end_s, end_g, end_out = [x1, attn], [s_out, gate[0]], [xn2, gate[1]], [x_in, x2[0]]
        end_tmp = attnT[:, :, :].rearrange("p k t -> p (k t)").rearrange("p (t d) -> p t d", t=T)
        hidden = probs_all[:, 0:FT * SLOTS].rearrange("p (f n) -> p f n", f=FT)

        score = [ctx.enter_context(nc.psum_tensor(f"score{b}", [P, 512], F32)) for b in range(3)]
        work = [ctx.enter_context(nc.psum_tensor(f"work{b}", [P, 512], F32)) for b in range(5)]
        ring = score + [work[4]]
        opsum = work[2:4]

        setup_in = sem("setup_in")
        setup_v = sem("setup_v")
        setup_a = sem("setup_a")
        setup_p = sem("setup_p")
        setup_t = sem("setup_t")
        zeroed = sem("zeroed")
        x_loaded = signal("x_loaded", 16)
        again_loaded = signal("again_loaded", 16)
        var_ready = signal("var_ready", 1)
        rstd_ready = signal("rstd_ready", 1)
        msq_ready = signal("msq_ready", 1)
        r1_ready = signal("r1_ready", 1)
        xn_ready = signal("xn_ready", 1)
        sq_ready = [signal(f"sq_ready{k}", 1) for k in range(2)]
        ss_ready = [signal(f"ss_ready{k}", 1) for k in range(2)]
        rn_ready = [signal(f"rn_ready{k}", 1) for k in range(2)]
        rope_pool = [signal(f"rope_pool{k}", 1) for k in range(2)]
        qn_ready = [signal(f"qn_ready{k}", 1) for k in range(2)]
        hi_ready = [signal(f"hi_ready{k}", 1) for k in range(2)]
        qkx_ready = [signal(f"qkx_ready{k}", 1) for k in range(2)]
        q_int_ready = signal("q_int_ready", 1)
        exp_y = signal("exp_y", 1)
        exp_y_capped = signal("exp_y_capped", 1)
        sig_ready = signal("sig_ready", 1)
        score_ready = Attending(sem("score_ready"), NCHUNK)
        exp_done = Attending(sem("exp_done"), NCHUNK)
        probs_masked = Attending(sem("probs_masked"), [STEPS_A, STEPS_A])
        pv_done = Attending(sem("pv_done"), [STEPS_A, STEPS_A])
        ss2_ready = signal("ss2_ready", 1)
        r2_ready = signal("r2_ready", 1)
        x1_ready = signal("x1_ready", 1)
        x1_stored = signal("x1_stored", 16 * 1)
        var2_ready = signal("var2_ready", 1)
        rstd2_ready = signal("rstd2_ready", 1)
        xn2_ready = signal("xn2_ready", 1)
        logit_e = signal("logit_e", 1)
        oh_ready = signal("oh_ready", 1)
        route_ready = signal("route_ready", 1)
        scattered = signal("scattered", 16 * T)
        routes_stored = signal("routes_stored", 16 * 2)
        skip_ready = signal("skip_ready", 1)
        hid_ready = signal("hid_ready", 2)
        s_stored = signal("s_stored", 16 * 1)
        work_made = [sem(f"work_made{b}") for b in range(5)]
        work_taken = [sem(f"work_taken{b}") for b in range(5)]
        w_loaded = pair("w_loaded", 2)
        rows_loaded = pair("rows_loaded", 1)
        rowsT_made = signal("rowsT_made", 2)
        rowsT_a = signal("rowsT_a", 1)
        rowsT_v = signal("rowsT_v", 1)
        hidden_made = signal("hidden_made", FT)
        relu_a = signal("relu_a", FT // 2)
        relu_v = signal("relu_v", FT // 2)
        down_made = signal("down_made", 2)
        down_taken = signal("down_taken", 2)
        rows_stored = pair("rows_stored", 1)
        g_loaded = pair("g_loaded", 4)
        g_gathered = pair("g_gathered", T)
        z_ready = signal("z_ready", 1)
        z_exp = signal("z_exp", 1)
        z_ln = signal("z_ln", 1)
        z_capped = signal("z_capped", 1)
        z_sig = signal("z_sig", 1)
        out_ready = signal("out_ready", 1)
        out_stored = pair("out_stored", 1)
        lru_ready = signal("lru_ready", KT)
        vf, vm, vb, vg, ve, vq = (Chain(sem(f"v_{n}")) for n in ("front", "between", "back", "gating", "ending", "quantize"))
        va = [Chain(sem(n)) for n in ("v_global", "v_local")]
        af, am, ab, ag = (Chain(sem(f"a_{n}")) for n in ("front", "between", "back", "gating"))
        pf, pm, pb, pa = (Chain(sem(f"p_{n}")) for n in ("front", "between", "back", "local"))
        v_end = Chain(sem("v_end"))

        def probs_view(kind, kb):
            w = width(kind, kb)
            return probs_all[:, probs_at[kb]:probs_at[kb] + GH * w].rearrange("p (h w) -> p h w", h=GH)

        def uses_before(name, s, plain=False):
            t = s - OFFSET_OF[name]
            uses = [(n, off) for n, off in BANK_USES[place(name)] if not (plain and n[0] == "O")]
            k = uses.index((name, OFFSET_OF[name]))
            if isinstance(s, int):
                return sum(turns_done(t, off) + (i < k and runs(t, off)) for i, (_, off) in enumerate(uses))
            return s * len(uses) + (k + sum(off for _, off in uses) - OFFSET_OF[name] * len(uses))

        def place(name):
            return BANK_OF[name]

        def rounds(s, kind):
            if kind == 0:
                return s - 1
            return min(s + 2, NSEQ) if isinstance(s, int) else s + 2

        def bank(name):
            return work[place(name)]

        def made(name):
            return work_made[place(name)]

        def taken(name):
            return work_taken[place(name)]

        def made_at(name, s):
            return uses_before(name, s, plain=True) + 1

        def taken_at(name, s):
            return uses_before(name, s) + 1

        def free_at(name, s):
            return uses_before(name, s)

        def used(name, s):
            return not isinstance(s, int) or uses_before(name, s) > 0

        def alone(eng):
            eng.nop(nofuse=True)

        def weave(*stages):
            heads = [[tick, n, g] for n, g in enumerate(stages) if (tick := next(g, None)) is not None]
            while heads:
                head = min(heads, key=lambda h: h[:2])
                tick, head[0] = head[0], next(head[2], None)
                if head[0] is None:
                    heads.remove(head)
                else:
                    assert head[0] >= tick

        def merged(*parts):
            heads = [[next(g), n, g] for n, g in enumerate(parts)]
            while heads:
                head = min(heads, key=lambda h: h[:2])
                yield head[0]
                head[0] = next(head[2], None)
                if head[0] is None:
                    heads.remove(head)

        def pipeline(eng, front, gating, attend_global, between, attend_local, ending, back):
            def turn(t, b):
                stages = ((ENDING, ending), (GLOBAL, attend_global), (BETWEEN, between), (GATE, gating), (BACK, back),
                          (LOCAL, attend_local), (FRONT, front))
                weave(*[stage(t + off, (b + off) % 2) for off, stage in stages if runs(t, off)])
            for t in range(-2, 2):
                turn(t, t % 2)
            with eng.Fori(1, NSEQ // 2 - 1) as i:
                turn(i * 2, 0)
                turn(i * 2 + 1, 1)
            for t in range(NSEQ - 2, NSEQ + 1):
                turn(t, t % 2)

        def sequences(eng, body):
            body(0, 0)
            body(1, 1)
            with eng.Fori(1, NSEQ // 2) as i:
                body(i * 2, 0)
                body(i * 2 + 1, 1)

        def experts(eng, body):
            body(0, 0)
            body(1, 1)
            with eng.Fori(1, E // 2) as i:
                body(i * 2, 0)
                body(i * 2 + 1, 1)

        block = ctx.enter_context(nc.Block())

        N_LOAD = 25
        V_ABS, V_ANGLE, V_NU, V_GAMMA, N_SETUP_V = 2, 23, 25, 52, 75

        @block.sync
        def _(sp):
            def load(dst, src):
                sp.dma_start(dst, src).then_inc(setup_in, 16)
            kxn = "(k p) n -> p k n"
            load(ident[:, :], a["c_ident"])
            load(had[:, :, :], a["c_had"].rearrange(kxn, p=P))
            load(upto[:, :], a["c_upto"])
            load(rope[:, :, :, :, :], a["c_rope"].rearrange("p (a b t d) -> p a b t d", a=2, b=2, t=T))
            load(small[:, :], a["c_small"])
            for b in range(2):
                load(normw[:, b, :], a[f"norm{b + 1}T"])
            load(wqkv[0][:, :, 0:D], a["L0_attn_g_wq"].rearrange(kxn, p=P))
            load(wqkv[1][:, :, 0:D], a["L0_attn_l_wq"].rearrange(kxn, p=P))
            load(wqkv[1][:, :, D:NQK], a["L0_attn_l_wk"].rearrange(kxn, p=P))
            load(wqkv[1][:, :, NQK:NQKV], a["L0_attn_l_wv"].rearrange(kxn, p=P))
            load(wo[0][:, :, :], a["L0_attn_g_wo"].rearrange(kxn, p=P))
            load(wo[1][:, :, :], a["L0_attn_l_wo"].rearrange(kxn, p=P))
            load(downT[0:LAT, :], a["downT"])
            load(ups[0:LAT, 0:64], a["L0_attn_g_k_up"])
            load(ups[0:LAT, 64:128], a["L0_attn_g_v_up"])
            load(tmp[0][:, 0:KT, :], a["ffn_wT"].rearrange(kxn, p=P))
            load(wr[:, :, :], a["L1_ffn_Wr"].rearrange(kxn, p=P))
            for c, n in enumerate(("re", "im")):
                load(bT[c][:, :, :], a[f"B_{n}T"].rearrange(kxn, p=P))
            load(cT[0][:, :, :], a["C_reT"].rearrange(kxn, p=P))
            load(cT[1][:, :, :], a["C_imT"].rearrange(kxn, p=P))
            load(dskip[:, :], a["D_skip"].partition_broadcast(P))
            load(lru_raw[:, :, :], a["lru_logs"].rearrange("p (a k) -> p a k", a=2))
            load(zT[:, 0, :], a["c_time"])

            def zero_slots(part):
                for n in range(part, (NSLOT + NTOK) // S, 2):
                    sp.dma_start(slots[n * S:(n + 1) * S, :].rearrange("(t p) d -> p t d", p=P),
                                 zeros[:, :].unsqueeze(1).broadcast_to([P, T, D])).then_inc(zeroed, 16)

            def turn(t):
                if runs(t, FRONT):
                    if runs(t, FRONT - 1):
                        sp.wait_ge(xn_ready.sem, xn_ready.at(t + FRONT - 1))
                    alone(sp)
                    sp.dma_start(x_in[:, :, :], rows(a["x"], t + FRONT)).then_inc(x_loaded.sem, 16)
                s = t + BACK
                if runs(t, BACK):
                    sp.wait_ge(x1_ready.sem, x1_ready.at(s))
                    alone(sp)
                    sp.dma_start(rows(kept_x, s), x1[:, :, :]).then_inc(x1_stored.sem, 16)
                if runs(t, 0):
                    if runs(t, BACK):
                        sp.wait_ge(xn2_ready.sem, xn2_ready.at(s))
                        alone(sp)
                        sp.wait_ge(x1_stored.sem, x1_stored.at(s))
                    alone(sp)
                    sp.dma_start(x1[:, :, :], rows(a["x"], t)).then_inc(again_loaded.sem, 16)
                if runs(t, BACK):
                    sp.wait_ge(route_ready.sem, route_ready.at(s))
                    alone(sp)
                    sp.dma_start(kept_idx[bass.ds(s * P, P), :], idx[0][:, :]).then_inc(routes_stored.sem, 16)
                    sp.dma_start(kept_fac[bass.ds(s * P, P), :], fac[0][:, :]).then_inc(routes_stored.sem, 16)
                    for n in range(2):
                        sp.wait_ge(taken(f"out{n}"), taken_at(f"out{n}", s))
                        alone(sp)
                    sp.dma_start(rows(kept_s, s), s_out[:, :, :]).then_inc(s_stored.sem, 16)

            turn(-2)
            sp.wait_ge(setup_p, 1)
            zero_slots(0)
            turn(-1)
            zero_slots(1)
            for t in range(0, 2):
                turn(t)
            with sp.Fori(1, NSEQ // 2 - 1) as i:
                turn(i * 2)
                turn(i * 2 + 1)
            for t in range(NSEQ - 2, NSEQ + 1):
                turn(t)

            sp.wait_ge(scattered.sem, scattered.at(NSEQ - 1))
            for stored in (x1_stored, s_stored, routes_stored):
                sp.wait_ge(stored.sem, stored.at(NSEQ - 1))

            def expert(e, b):
                if came(e, 2):
                    sp.wait_ge(down_made.sem, down_made.at((e - 1) * STEPS - 1))
                sp.dma_start(w1[b][:, :, :], w1_rows(e)).then_inc(w_loaded.sems[b], 16)
                sp.dma_start(w2[b][:, :, :], w2_rows(e)).then_inc(w_loaded.sems[b], 16)
                for j in range(STEPS):
                    n, nb = e * STEPS + j, (b * STEPS + j) % 2
                    if rowsT_made.was(n, lag=2):
                        sp.wait_ge(rowsT_made.sem, rowsT_made.before(n, lag=2))
                    sp.dma_start(rows_in[nb][:, :, :], slot_rows(n)).then_inc(rows_loaded.sems[nb], 16)
                    if came(n):
                        store_rows(n - 1, 1 - nb)

            def store_rows(n, nb):
                sp.wait_ge(down_taken.sem, down_taken.at(n))
                sp.dma_start(slot_rows(n), rows_out[nb][:, :, :]).then_inc(rows_stored.sems[nb], 16)
            experts(sp, expert)
            store_rows(E * STEPS - 1, (E * STEPS - 1) % 2)

            def last_part(s, b):
                if out_ready.was(s, lag=2):
                    sp.wait_ge(out_ready.sem, out_ready.before(s, lag=2))
                sp.dma_start(end_x1[b][:, :, :], rows(kept_x, s)).then_inc(g_loaded.sems[b], 16)
                sp.dma_start(end_s[b][:, :, :], rows(kept_s, s)).then_inc(g_loaded.sems[b], 16)
                sp.dma_start(idx[b][:, :], kept_idx[bass.ds(s * P, P), :]).then_inc(g_loaded.sems[b], 16)
                sp.dma_start(fac[b][:, :], kept_fac[bass.ds(s * P, P), :]).then_inc(g_loaded.sems[b], 16)
                if came(s):
                    store_out(s - 1, 1 - b)

            def store_out(s, b):
                sp.wait_ge(out_ready.sem, out_ready.at(s))
                sp.dma_start(rows(out, s), end_out[b][:, :, :]).then_inc(out_stored.sems[b], 16)
            for stored in (x1_stored, s_stored, routes_stored):
                sp.wait_ge(stored.sem, stored.at(NSEQ - 1))
            sequences(sp, last_part)
            store_out(NSEQ - 1, 1)
            for b in range(2):
                sp.wait_ge(out_stored.sems[b], out_stored.total(NSEQ))

        @block.gpsimd
        def _(pool):
            pool.memset(zeros[:, :], 0.0).then_inc(setup_p, 1)
            for k in range(2):
                pool.memset(kT[k][:, :, :, :, :], 0.0).then_inc(setup_p, 1)
                pool.memset(v_sb[k][:, :, :, :], 1.0).then_inc(setup_p, 1)
            pool.memset(v_sb[2][:, :, :, :], 1.0).then_inc(setup_p, 1)
            pool.memset(qx[:, :, :, :], 0.0).then_inc(setup_p, 1)
            pool.memset(kx[:, :, :, :, :], 0.0).then_inc(setup_p, 1)
            pool.memset(ones_bf[:, :], 1.0).then_inc(setup_p, 1)
            pool.memset(ones[:, :], 1.0).then_inc(setup_p, 1)
            for c, val in enumerate((1e-5, 1e-6, np.pi / 2, 1.0)):
                pool.memset(eps[:, c:c + 1], float(val)).then_inc(setup_p, 1)
            pool.memset(base[:, :], 0.0).then_inc(setup_p, 1)
            pool.wait_ge(setup_v, N_SETUP_V)

            def rope_half(s, kind):
                for t in (2, 3):
                    pool.wait_ge(taken(f"p{kind}_{t}"), taken_at(f"p{kind}_{t}", s))
                if came(s, 2 - 2 * kind):
                    pool.wait_ge(qn_ready[1 - kind].sem, rounds(s, kind))
                pairs = qk[:, :, :].rearrange("p t (h d two) -> p t h d two", h=H + KVH, two=2)
                for j, (part, trig) in enumerate(((0, 1), (1, 0))):
                    table = rope[:, kind, trig].unsqueeze(2).broadcast_to([P, T, H + KVH, HD // 2])
                    ins = pool.tensor_tensor(
                        ropetmp[2 + j][:, :, :].rearrange("p t (h d) -> p t h d", h=H + KVH),
                        pairs[:, :, :, :, part], table, ALU.mult)
                    if j == 0:
                        (pm if kind else pf).inc(ins)
                    else:
                        ins.then_inc(rope_pool[kind].sem, 1)

            def front(s, b):
                yield 31
                pf.start(s)
                rope_half(s, 0)

            def between(s, b):
                yield 10
                pm.start(s)
                rope_half(s, 1)

            def nothing(s, b):
                return iter(())

            def attend(s, kind):
                yield LOCAL_AT * kind
                if kind:
                    pa.start(s)
                chunk = 0
                for g in range(KVH):
                    for kb in range(T):
                        yield LOCAL_AT * kind + STEP * (g * T + kb)
                        chunk += len(chunks(kind, kb))
                        w = width(kind, kb)
                        pool.wait_ge(exp_done.sem, exp_done.at(s, kind, chunk))
                        alone(pool)
                        pr = probs_view(kind, kb)
                        tri = pool.affine_select(out=pr[:, :, 0:P], in_=pr[:, :, 0:P], compare_op=ALU.is_ge, fill=0.0,
                                                 base=0, pattern=[[0, GH], [1, P]], channel_multiplier=-1)
                        if kind == 1:
                            pa.inc(tri)
                            pool.wait_ge(pa.sem, pa.at())
                            alone(pool)
                            n = w - WIN
                            tri = pool.affine_select(out=pr[:, :, WIN:w], in_=pr[:, :, WIN:w], compare_op=ALU.is_ge,
                                                     fill=0.0, base=-1, pattern=[[0, GH], [-1, n]],
                                                     channel_multiplier=1)
                        tri.then_inc(probs_masked.sem, 1)

            def back(s, b):
                yield 23
                pb.start(s)
                pool.wait_ge(xn2_ready.sem, xn2_ready.at(s))
                if s_stored.was(s):
                    pool.wait_ge(s_stored.sem, s_stored.before(s))
                pool.tensor_tensor(s_out[:, :, :], xn2[:, :, :],
                                   dskip[:, :].unsqueeze(1).broadcast_to([P, T, D]), ALU.mult).then_inc(skip_ready.sem, 1)
                yield 30
                pool.wait_ge(route_ready.sem, route_ready.at(s))
                if not came(s):
                    pool.wait_ge(zeroed, 16 * ((NSLOT + NTOK) // S))
                alone(pool)
                for t in range(T):
                    yield 31 + t
                    pool.indirect_dma_start(
                        slots[:, :], bass.IndirectOffsetOnAxis(ap=idx[0][:, t:t + 1], axis=0),
                        xn2[:, t, :], None).then_inc(scattered.sem, 16)
                for h in range(KT):
                    yield 35 + 10 * h
                    pool.wait_ge(lru_ready.sem, lru_ready.at(s, h + 1))
                    if h == 0 and came(s):
                        pool.wait_ge(made("out1"), made_at("out1", s - 1))
                    pb.inc(pool.tensor_tensor(hid[0][h][:, :], lru[0], lru[1], ALU.subtract))
                    pool.tensor_tensor(hid[1][h][:, :], lru[2], lru[3], ALU.add).then_inc(hid_ready.sem, 1)
            pipeline(pool, front, nothing, lambda s, b: attend(s, 0), between, lambda s, b: attend(s, 1), nothing, back)

            for b in range(2):
                pool.wait_ge(rows_stored.sems[b], rows_stored.total(E * STEPS))

            def gather(s, b):
                pool.wait_ge(g_loaded.sems[b], g_loaded.at(s, b))
                if out_ready.was(s, lag=2):
                    pool.wait_ge(out_ready.sem, out_ready.before(s, lag=2))
                alone(pool)
                for t in range(T):
                    pool.indirect_dma_start(
                        end_g[b][:, t, :], None, slots[:, :],
                        bass.IndirectOffsetOnAxis(ap=idx[b][:, t:t + 1], axis=0)).then_inc(g_gathered.sems[b], 16)
            sequences(pool, gather)

        @block.tensor
        def _(pe):
            mm = pe.matmul
            pe.wait_ge(setup_in, 16 * N_LOAD)
            pe.wait_ge(setup_p, 10)
            for k in range(KT):
                last = mm(work[0][:, k * P:(k + 1) * P], downT[0:LAT, k * P:(k + 1) * P], ups[0:LAT, :],
                          start=True, stop=True)
            last.then_inc(setup_t, 1)
            pe.wait_ge(setup_v, V_ABS)
            for k in range(KT):
                last = mm(work[1][:, 0:D], ones[:, :], tmp[1][:, k, :], start=(k == 0), stop=(k == KT - 1))
            last.then_inc(setup_t, 1)
            pe.wait_ge(setup_v, N_SETUP_V)

            def transposes(s, src_at, names):
                for k, name in enumerate(names):
                    if used(name, s):
                        pe.wait_ge(taken(name), free_at(name, s))
                    w = bank(name)
                    for t in range(T):
                        last = pe.transpose(w[:, t * P:(t + 1) * P], src_at(t, k), ident[:, :])
                    last.then_inc(made(name), 1)

            def token_major(s, name, lhs, rhs, tiles, n):
                if used(name, s):
                    pe.wait_ge(taken(name), free_at(name, s))
                w = bank(name)
                for j, t in enumerate(tiles):
                    for k in range(len(lhs)):
                        last = mm(w[:, j * n:(j + 1) * n], lhs[k](t), rhs[k], start=(k == 0), stop=(k == len(lhs) - 1))
                last.then_inc(made(name), 1)

            def tok(buf, t):
                return buf[:, t * P:(t + 1) * P]

            def tiles(buf):
                return [lambda t, k=k: tok(buf[:, k, :], t) for k in range(KT)]

            def qk_transposes(s, kind):
                for half in range(2):
                    name = f"k{kind}_{half}"
                    yield TICK[name]
                    if half == 0:
                        pe.wait_ge(qkx_ready[kind].sem, qkx_ready[kind].at(s))
                    if used(name, s):
                        pe.wait_ge(taken(name), free_at(name, s))
                    w = bank(name)[:, :].bitcast(F16)
                    for j in range(8):
                        t, g = 2 * half + j // KVH, j % KVH
                        last = pe.transpose(w[:, j * P:(j + 1) * P],
                                            kx[:, t, g].rearrange("p two d -> p (two d)"), ident_h[:, :])
                    last.then_inc(made(name), 1)
                for qr in range(4):
                    name = f"q{kind}_{qr}"
                    yield TICK[name]
                    if used(name, s):
                        pe.wait_ge(taken(name), free_at(name, s))
                    w = bank(name)[:, :].bitcast(F16)
                    for j in range(8):
                        pair_, t = 2 * qr + j // T, j % T
                        last = pe.transpose(w[:, j * P:(j + 1) * P],
                                            qx[:, t, 2 * pair_:2 * pair_ + 2].rearrange("p h d -> p (h d)"), ident_h[:, :])
                    last.then_inc(made(name), 1)

            def attend(s, b, kind):
                yield LOCAL_AT * kind
                for n in (2, 3):
                    name = f"q{kind}_{n}"
                    pe.wait_ge(taken(name), taken_at(name, s))
                chunk = [0]

                def scores(g, kb):
                    w = width(kind, kb)
                    for h0, heads in chunks(kind, kb):
                        c = chunk[0]
                        if exp_done.was(s, kind, max(c - 2, 0)):
                            pe.wait_ge(exp_done.sem, exp_done.at(s, kind, max(c - 2, 0)))
                        for n in range(heads):
                            h = GH * g + h0 + n
                            o = score[(c + kind * NCHUNK[0]) % 3][:, n * w:(n + 1) * w]
                            last = mm(o, kT[kind][:, h % 2, kb, g, :], qT[kind][:, h // 2, kb * P:kb * P + w],
                                      start=True, stop=True)
                        last.then_inc(score_ready.sem, 1)
                        chunk[0] += 1

                for n, (g, kb) in enumerate(STEP_ORDER):
                    if n:
                        yield LOCAL_AT * kind + STEP * n
                    scores(g, kb)
                    if n >= LAG:
                        weighted(s, b, kind, *STEP_ORDER[n - LAG])
                    if kb == 3 and g:
                        to_tokens(s, kind, g - 1)
                if kind == 0:
                    yield from finish(s, b, kind, LOCAL_AT)

            def weighted(s, b, kind, g, kb):
                n = g * T + kb
                name = f"O{kind}_{g}"
                pe.wait_ge(probs_masked.sem, probs_masked.at(s, kind, n + 1))
                if kb == 0 and used(name, s):
                    pe.wait_ge(taken(name), free_at(name, s))
                w = width(kind, kb)
                pr = probs_view(kind, kb)
                for lo, hi in [(0, w)] if kind == 0 or kb == 0 else [(0, WIN), (WIN, w)]:
                    for j in range(GH):
                        last = mm(bank(name)[32 * j:32 * j + 32, kb * P + lo:kb * P + hi], v_sb[2 if kind else b][:, kb, g, :],
                                  pr[:, j, lo:hi], start=(kb == 0), stop=(kb == T - 1 and hi == w))
                last.then_inc(pv_done.sem, 1)

            def to_tokens(s, kind, g):
                name = f"r{kind}_{g}"
                pe.wait_ge(taken(name), free_at(name, s))
                for t in range(T):
                    last = pe.transpose(bank(name)[:, t * P:(t + 1) * P], oT[g % 2][:, t * P:(t + 1) * P], ident[:, :])
                last.then_inc(made(name), 1)

            def finish(s, b, kind, tick):
                for n in range(LAG):
                    yield tick + STEP * n
                    weighted(s, b, kind, *STEP_ORDER[STEPS_A - LAG + n])
                yield tick + 6
                to_tokens(s, kind, KVH - 1)
                yield TICK[f"a{kind}_0"]
                for g in (2, 3):
                    name = f"r{kind}_{g}"
                    pe.wait_ge(taken(name), taken_at(name, s))
                transposes(s, lambda t, k: attn[:, t, k * P:(k + 1) * P], [f"a{kind}_0", f"a{kind}_1"])
                for n in range(2):
                    yield TICK[f"o{kind}_{n}"]
                    if n == 0:
                        for k in range(KT):
                            pe.wait_ge(taken(f"a{kind}_{k}"), taken_at(f"a{kind}_{k}", s))
                    token_major(s, f"o{kind}_{n}", tiles(attnT),
                                [wo[kind][:, k, :] for k in range(KT)], [2 * n, 2 * n + 1], D)

            def ending(s, b):
                yield from finish(s, b, 1, 0)

            def project(s, kind, x):
                for t in range(T):
                    yield TICK[f"p{kind}_{t}"]
                    if t == 0:
                        for k in range(KT):
                            pe.wait_ge(taken(f"{x}{k}"), taken_at(f"{x}{k}", s))
                    token_major(s, f"p{kind}_{t}", tiles(xT), [wqkv[kind][:, k, :] for k in range(KT)], [t], NQKV)

            def front(s, b):
                yield TICK["xT0"]
                pe.wait_ge(xn_ready.sem, xn_ready.at(s))
                transposes(s, lambda t, k: xn[b][:, t, k * P:(k + 1) * P], ["xT0", "xT1"])
                yield from project(s, 0, "xT")
                for n in range(2):
                    yield TICK[f"had{n}"]
                    token_major(s, f"had{n}", tiles(xT), [had[:, k, :] for k in range(KT)], [2 * n, 2 * n + 1], D)
                yield TICK["qT"]
                pe.wait_ge(q_int_ready.sem, q_int_ready.at(s))
                if used("qT", s):
                    pe.wait_ge(taken("qT"), free_at("qT", s))
                w = bank("qT")[:, :].bitcast(BF16)
                for j in range(KT * T):
                    k, t = j // T, j % T
                    last = pe.transpose(w[:, j * P:(j + 1) * P], q_int[:, t, k * P:(k + 1) * P], ident_bf[:, :])
                last.then_inc(made("qT"), 1)
                yield from qk_transposes(s, 0)

            def gating(s, b):
                for n in range(2):
                    yield TICK[f"ffn{n}"]
                    pe.wait_ge(taken("qT"), taken_at("qT", s))
                    token_major(s, f"ffn{n}", tiles(q_intT), [ternT[:, k, :] for k in range(KT)], [2 * n, 2 * n + 1], D)

            def between(s, b):
                yield TICK["yT0"]
                for n in range(2):
                    pe.wait_ge(taken(f"o0_{n}"), taken_at(f"o0_{n}", s))
                transposes(s, lambda t, k: x2[b][:, t, k * P:(k + 1) * P], ["yT0", "yT1"])
                yield from project(s, 1, "yT")
                yield from qk_transposes(s, 1)

            def recurrence_inputs(s, h):
                for c in range(2):
                    name = f"u{h}_{c}"
                    if used(name, s):
                        pe.wait_ge(taken(name), free_at(name, s))
                    w = bank(name)
                    for k in range(KT):
                        last = mm(w[:, :], bT[c][:, k, h * P:(h + 1) * P], zT[:, k, :], start=(k == 0), stop=(k == KT - 1))
                    last.then_inc(made(name), 1)

            def back(s, b):
                yield TICK["zT0"]
                pe.wait_ge(xn2_ready.sem, xn2_ready.at(s))
                transposes(s, lambda t, k: xn2[:, t, k * P:(k + 1) * P], ["zT0", "zT1"])
                yield TICK["logit"]
                for k in range(KT):
                    pe.wait_ge(taken(f"zT{k}"), taken_at(f"zT{k}", s))
                token_major(s, "logit", tiles(zT), [wr[:, k, :] for k in range(KT)], range(T), E)
                yield TICK["count"]
                if used("count", s):
                    pe.wait_ge(taken("count"), free_at("count", s))
                w = bank("count")
                pe.wait_ge(oh_ready.sem, oh_ready.at(s))
                for t in range(T):
                    for q in range(t + 1):
                        mm(w[:, t * E:(t + 1) * E], upto_bf[:, :] if q == t else ones_bf[:, :], oh_bf[:, q, :],
                           start=(q == 0), stop=(q == t))
                for q in range(T):
                    last = mm(w[:, T * E:(T + 1) * E], ones_bf[:, :], oh_bf[:, q, :], start=(q == 0), stop=(q == T - 1))
                last.then_inc(made("count"), 1)
                yield TICK["u0_0"]
                recurrence_inputs(s, 0)
                yield TICK["u1_0"]
                recurrence_inputs(s, 1)
                for n in range(2):
                    yield TICK[f"out{n}"]
                    pe.wait_ge(hid_ready.sem, hid_ready.at(s))
                    token_major(s, f"out{n}", [lambda t, c=c, k=k: tok(hid[c][k], t) for c in range(2) for k in range(KT)],
                                [cT[c][:, k, :] for c in range(2) for k in range(KT)], [2 * n, 2 * n + 1], D)
            pipeline(pe, front, gating, lambda s, b: attend(s, b, 0), between, lambda s, b: attend(s, b, 1), ending, back)

            def row_transposes(n, nb):
                pe.wait_ge(rows_loaded.sems[nb], rows_loaded.at(n, nb))
                for k in range(KT):
                    if (rowsT_v if k else rowsT_a).was(n):
                        pe.wait_ge((rowsT_v if k else rowsT_a).sem, (rowsT_v if k else rowsT_a).before(n))
                    for t in range(T):
                        last = pe.transpose(work[k][:, t * P:(t + 1) * P], rows_in[nb][:, t, k * P:(k + 1) * P], ident[:, :])
                    last.then_inc(rowsT_made.sem, 1)

            def expert(e, b):
                pe.wait_ge(w_loaded.sems[b], w_loaded.at(e, b))
                for j in range(STEPS):
                    n, nb = e * STEPS + j, (b * STEPS + j) % 2
                    if j == 0:
                        row_transposes(n, nb)
                    pe.wait_ge(rowsT_a.sem, rowsT_a.at(n))
                    pe.wait_ge(rowsT_v.sem, rowsT_v.at(n))
                    for f in range(FT):
                        if (relu_v if f % 2 else relu_a).was(n, f // 2 - 1):
                            pe.wait_ge((relu_v if f % 2 else relu_a).sem, (relu_v if f % 2 else relu_a).before(n, f // 2 - 1))
                        o = ring[f % 4][:, :]
                        for k in range(KT):
                            last = mm(o, w1[b][:, k, f * P:(f + 1) * P], rowsT[nb][:, k, :], start=(k == 0), stop=(k == KT - 1))
                        last.then_inc(hidden_made.sem, 1)
                    if j < STEPS - 1:
                        row_transposes(n + 1, 1 - nb)
                    pe.wait_ge(relu_a.sem, relu_a.at(n))
                    pe.wait_ge(relu_v.sem, relu_v.at(n))
                    for m in range(2):
                        if down_taken.was(n, m):
                            pe.wait_ge(down_taken.sem, down_taken.before(n, m))
                        for t in (2 * m, 2 * m + 1):
                            for f in range(FT):
                                last = mm(opsum[m][:, (t % 2) * D:(t % 2 + 1) * D], hidden[:, f, t * P:(t + 1) * P],
                                          w2[b][:, f, :], start=(f == 0), stop=(f == FT - 1))
                        last.then_inc(down_made.sem, 1)
            experts(pe, expert)

        @block.scalar
        def _(act):
            f = act.activation

            def chained(chain, ins, wait=True):
                chain.inc(ins)
                if wait:
                    act.wait_ge(chain.sem, chain.at())

            act.wait_ge(setup_in, 16 * N_LOAD)
            f(lru_raw[:, :, :], lru_raw[:, :, :], ACT.Exp).then_inc(setup_a, 1)
            act.wait_ge(setup_v, V_ANGLE)
            f(sinT[:, :, :], sinT[:, :, :], ACT.Sin).then_inc(setup_a, 1)
            f(cosT[:, :, :], cosT[:, :, :], ACT.Sin).then_inc(setup_a, 1)
            act.preload_act_table_set("natural_log_exp_and_others")
            act.wait_ge(setup_v, V_NU)
            f(sc[:, 2:4, 0], sc[:, 2:4, 0], ACT.Exp, scale=-1.0).then_inc(setup_a, 1)
            f(sc[:, 4:6, 0], sc[:, 4:6, 0], ACT.Exp, scale=-1.0).then_inc(setup_a, 1)
            act.wait_ge(setup_v, V_GAMMA)
            f(sc[:, 6:8, 0], sc[:, 6:8, 0], ACT.Ln, bias=eps[:, 0:1]).then_inc(setup_a, 1)
            act.wait_ge(setup_a, 6)
            f(sc[:, 6:8, 0], sc[:, 6:8, 0], ACT.Exp, scale=0.5).then_inc(setup_a, 1)
            act.wait_ge(setup_v, N_SETUP_V)

            def rsqrt(chain, dst, src, bias, scale=1.0, tmp_=None):
                chained(chain, f(tmp_, src, ACT.Ln, bias=bias, scale=scale))
                return f(dst, tmp_, ACT.Exp, scale=-0.5)

            def prepare_qk(s, kind, chain, r, v_at):
                for t in range(T):
                    name = f"p{kind}_{t}"
                    yield TICK[name] + 1
                    act.wait_ge(made(name), made_at(name, s))
                    if t == 0:
                        if came(s, 2 - 2 * kind):
                            act.wait_ge(qn_ready[1 - kind].sem, rounds(s, kind))
                        if came(s, 2 - 2 * kind):
                            act.wait_ge(ss_ready[1 - kind].sem, rounds(s, kind))
                        if came(s, 2 - kind):
                            act.wait_ge(pv_done.sem, pv_done.at(s - 2 + kind, kind, STEPS_A))
                    chained(chain, f(qk[:, t, :], bank(name)[:, 0:NQK], ACT.Copy, scale=r[:, t:t + 1]), wait=False)
                    f(v_at[:, t, :, 0:HD], bank(name)[:, NQK:NQKV].rearrange("p (g d) -> p g d", g=KVH), ACT.Copy,
                      scale=r[:, t:t + 1]).then_inc(taken(name), 1)
                yield TICK[name] + (3 if kind else 2)
                act.wait_ge(taken(name), taken_at(name, s))
                if came(s, 2 - 2 * kind):
                    act.wait_ge(qkx_ready[1 - kind].sem, rounds(s, kind))
                f(rot[:, :, :], qk[:, :, :], ACT.Square).then_inc(sq_ready[kind].sem, 1)
                yield TICK[name] + (7 if kind else 6)
                act.wait_ge(ss_ready[kind].sem, ss_ready[kind].at(s))
                rsqrt(chain, nrm[:, 1, :], nrm[:, 0, :], eps[:, 1:2], 1.0 / HD, nrm[:, 1, :]).then_inc(rn_ready[kind].sem, 1)
                yield TICK[name] + (11 if kind else 10)
                act.wait_ge(qn_ready[kind].sem, qn_ready[kind].at(s))
                if kind:
                    after = min(s + 1, NSEQ - 1) if isinstance(s, int) else s + 1
                    act.wait_ge(taken("q0_3"), taken_at("q0_3", after))
                elif came(s, 2):
                    act.wait_ge(taken("q1_3"), taken_at("q1_3", s - 2))
                rv = rot[:, :, :].rearrange("p t (h d) -> p t h d", h=H + KVH)
                for c in range(2):
                    for part in (0, 32):
                        chained(chain, f(kx[:, :, :, c, part:part + HD], rv[:, :, H:, :], ACT.Copy), wait=False)
                chained(chain, f(qx[:, :, :, 0:HD], rv[:, :, 0:H, :], ACT.Copy), wait=False)
                f(qx[:, :, :, HD:2 * HD], rv[:, :, 0:H, :], ACT.Copy).then_inc(hi_ready[kind].sem, 1)

            def attend(s, kind):
                chunk = 0
                for g in range(KVH):
                    for kb in range(T):
                        yield LOCAL_AT * kind + STEP * (g * T + kb)
                        w = width(kind, kb)
                        pr = probs_view(kind, kb)
                        n = g * T + kb
                        if pv_done.was(s, kind, n - T + 1):
                            act.wait_ge(pv_done.sem, pv_done.at(s, kind, n - T + 1))
                        for h0, heads in chunks(kind, kb):
                            act.wait_ge(score_ready.sem, score_ready.at(s, kind, chunk + 1))
                            f(pr[:, h0:h0 + heads, :].rearrange("p h w -> p (h w)"),
                              score[(chunk + kind * NCHUNK[0]) % 3][:, 0:heads * w], ACT.Exp, scale=HD ** -0.5).then_inc(exp_done.sem, 1)
                            chunk += 1
                        if kb == LAG - 1 and g:
                            take_sums(s, kind, g - 1)
                if kind == 0:
                    yield from finish(s, kind, LOCAL_AT)

            def finish(s, kind, tick):
                yield tick + 5
                take_sums(s, kind, KVH - 1)

            def ending(s, b):
                yield from finish(s, 1, 0)

            def take_sums(s, kind, g):
                act.wait_ge(pv_done.sem, pv_done.at(s, kind, g * T + T))
                f(oT[g % 2][:, :], bank(f"O{kind}_{g}")[:, :], ACT.Copy).then_inc(taken(f"O{kind}_{g}"), 1)

            def front(s, b):
                yield 13
                af.start(s)
                act.wait_ge(var_ready.sem, var_ready.at(s))
                rsqrt(af, sc[:, RSTD], mv[0][:, :, 1], eps[:, 0:1], 1.0, sc[:, LN]).then_inc(rstd_ready.sem, 1)
                yield 16
                act.wait_ge(msq_ready.sem, msq_ready.at(s))
                rsqrt(af, sc[:, R1], sc[:, M2], eps[:, 1:2], 1.0, sc[:, LN]).then_inc(r1_ready.sem, 1)
                yield TICK["xT0"] + 1
                act.wait_ge(r1_ready.sem, r1_ready.at(s))
                act.wait_ge(made("xT0"), made_at("xT0", s))
                f(xT[:, 0, :], bank("xT0")[:, :], ACT.Copy).then_inc(taken("xT0"), 1)
                yield from prepare_qk(s, 0, af, sc[:, R1], v_sb[b])

            def gating(s, b):
                yield 15
                ag.start(s)
                for n in range(2):
                    act.wait_ge(taken(f"ffn{n}"), taken_at(f"ffn{n}", s))
                f(tmp[1][:, :, :], tmp[0][:, :, :], ACT.Exp, scale=-1.0).then_inc(exp_y.sem, 1)
                yield 19
                act.wait_ge(exp_y_capped.sem, exp_y_capped.at(s))
                chained(ag, f(tmp[1][:, :, :], tmp[1][:, :, :], ACT.Ln, bias=eps[:, 3:4]))
                f(tmp[1][:, :, :], tmp[1][:, :, :], ACT.Exp, scale=-1.0).then_inc(sig_ready.sem, 1)

            def between(s, b):
                yield 0
                am.start(s)
                for n in range(2):
                    act.wait_ge(taken(f"o0_{n}"), taken_at(f"o0_{n}", s))
                act.wait_ge(qkx_ready[0].sem, rounds(s, 1))
                for t in range(T):
                    chained(am, f(rot[:, t, 0:D], x2[b][:, t, :], ACT.Square, accum_out=sc[:, SS2, t:t + 1]), wait=(t == T - 1))
                rsqrt(am, sc[:, R2], sc[:, SS2], eps[:, 1:2], 1.0 / D, sc[:, LN2]).then_inc(r2_ready.sem, 1)
                yield 1
                act.wait_ge(made("yT0"), made_at("yT0", s))
                f(xT[:, 0, :], bank("yT0")[:, :], ACT.Copy).then_inc(taken("yT0"), 1)
                act.wait_ge(r2_ready.sem, r2_ready.at(s))
                yield from prepare_qk(s, 1, am, sc[:, R2], v_sb[2])

            def back(s, b):
                yield 17
                ab.start(s)
                act.wait_ge(var2_ready.sem, var2_ready.at(s))
                rsqrt(ab, sc[:, RSTD2], mv[1][:, :, 1], eps[:, 0:1], 1.0, sc[:, LN3]).then_inc(rstd2_ready.sem, 1)
                yield TICK["zT0"] + 1
                act.wait_ge(made("zT0"), made_at("zT0", s))
                f(zT[:, 0, :], bank("zT0")[:, :], ACT.Copy).then_inc(taken("zT0"), 1)
                yield 26
                act.wait_ge(taken("logit"), taken_at("logit", s))
                f(lg[:, 4], lg[:, 3], ACT.Exp).then_inc(logit_e.sem, 1)
            pipeline(act, front, gating, lambda s, b: attend(s, 0), between, lambda s, b: attend(s, 1), ending, back)

            def take_rowsT(n, nb):
                act.wait_ge(rowsT_made.sem, rowsT_made.at(n, 1))
                f(rowsT[nb][:, 0, :], work[0][:, :], ACT.Copy).then_inc(rowsT_a.sem, 1)

            def expert(e, b):
                for j in range(STEPS):
                    n, nb = e * STEPS + j, (b * STEPS + j) % 2
                    if j == 0:
                        take_rowsT(n, nb)
                    for g in range(0, FT, 2):
                        act.wait_ge(hidden_made.sem, hidden_made.at(n, g + 1))
                        if g == 0:
                            if down_made.was(n):
                                act.wait_ge(down_made.sem, down_made.before(n))
                        f(hidden[:, g, :], ring[g % 4][:, :], ACT.Relu).then_inc(relu_a.sem, 1)
                    if j < STEPS - 1:
                        take_rowsT(n + 1, 1 - nb)
                    for m in range(2):
                        act.wait_ge(down_made.sem, down_made.at(n, m + 1))
                        if m == 0:
                            if came(n, 2):
                                act.wait_ge(rows_stored.sems[nb], rows_stored.at(n - 2, nb))
                        f(rows_out[nb][:, 2 * m:2 * m + 2, :].rearrange("p t d -> p (t d)"), opsum[m][:, :],
                          ACT.Copy).then_inc(down_taken.sem, 1)
            experts(act, expert)

            def last_part(s, b):
                act.wait_ge(z_ready.sem, z_ready.at(s))
                f(tmp[1][:, :, :], tmp[0][:, :, :], ACT.Exp, scale=-1.0).then_inc(z_exp.sem, 1)
                act.wait_ge(z_capped.sem, z_capped.at(s))
                f(tmp[2][:, :, :], tmp[1][:, :, :], ACT.Ln, bias=eps[:, 3:4]).then_inc(z_ln.sem, 1)
                act.wait_ge(z_ln.sem, z_ln.at(s))
                f(tmp[1][:, :, :], tmp[2][:, :, :], ACT.Exp, scale=-1.0).then_inc(z_sig.sem, 1)
            sequences(act, last_part)

        @block.vector
        def _(v):
            tt, ts, stt = v.tensor_tensor, v.tensor_scalar, v.scalar_tensor_tensor

            def chained(chain, ins, wait=True):
                chain.inc(ins)
                if wait:
                    v.wait_ge(chain.sem, chain.at())

            n_done = [0]

            def step(ins):
                n_done[0] += 1
                ins.then_inc(setup_v, 1)
                v.wait_ge(setup_v, n_done[0])
                return n_done[0]

            v.wait_ge(setup_in, 16 * N_LOAD)
            v.wait_ge(setup_p, 15)
            assert step(ts(tmp[1][:, 0:KT, :], tmp[0][:, 0:KT, :], -1.0, None, ALU.mult)) == 1
            assert step(tt(tmp[1][:, 0:KT, :], tmp[1][:, 0:KT, :], tmp[0][:, 0:KT, :], ALU.max)) == V_ABS
            v.wait_ge(setup_a, 1)
            theta = lru_raw[:, 1, :]

            def reduce_angle(x, k):
                c1 = 6.28125
                c2 = float(np.float32(np.round((TWO_PI - c1) * 2 ** 21) / 2 ** 21))
                c3 = float(TWO_PI - c1 - c2)
                step(ts(k, x, 1.0 / TWO_PI, MAGIC, ALU.mult, ALU.add))
                step(ts(k, k, -MAGIC, None, ALU.add))
                for c in (c1, c2, c3):
                    step(stt(x, k, -c, x, ALU.mult, ALU.add))
                step(ts(x, x, float(np.float32(3.1415925)), float(np.float32(-3.1415925)), ALU.min, ALU.max))
            reduce_angle(theta, sc[:, 0:KT, 0])
            for k in range(KT):
                step(ts(sinT[:, k, :], zT[:, 0, :], lru_raw[:, 1, k:k + 1], None, ALU.mult))
            reduce_angle(sinT[:, :, :], attnT[:, :, :])
            step(ts(cosT[:, :, :], sinT[:, :, :], float(np.pi / 2), None, ALU.add))
            reduce_angle(cosT[:, :, :], attnT[:, :, :])
            assert n_done[0] == V_ANGLE, n_done
            nus = lru_raw[:, 0, :]
            step(v.tensor_copy(sc[:, 2:4, 0], nus))
            assert step(ts(sc[:, 4:6, 0], nus, 2.0, None, ALU.mult)) == V_NU
            step(v.tensor_copy(sc[:, 8:10, 0], nus))
            step(ts(sc[:, 10:12, 0], nus, 2.0, None, ALU.mult))
            y = sc[:, 8:12, 0]
            ycap = sc[:, 12:16, 0]
            ser = sc[:, 16:20, 0]
            big = sc[:, 20:24, 0]
            step(ts(ycap, y, 0.5, None, ALU.min))
            step(ts(ser, ycap, -1.0 / 10, 1.0, ALU.mult, ALU.add))
            for n in range(9, 1, -1):
                step(tt(ser, ser, ycap, ALU.mult))
                step(ts(ser, ser, -1.0 / n, 1.0, ALU.mult, ALU.add))
            step(tt(ser, ser, ycap, ALU.mult))
            step(ts(big, y, 0.5, None, ALU.is_gt))
            v.wait_ge(setup_a, 5)
            step(ts(sc[:, 2:6, 0], sc[:, 2:6, 0], -1.0, 1.0, ALU.mult, ALU.add))
            step(tt(sc[:, 2:6, 0], sc[:, 2:6, 0], ser, ALU.subtract))
            step(tt(sc[:, 2:6, 0], sc[:, 2:6, 0], big, ALU.mult))
            step(tt(ser, ser, sc[:, 2:6, 0], ALU.add))
            gamma_at = step(v.tensor_copy(sc[:, 6:8, 0], sc[:, 18:20, 0]))
            assert gamma_at == V_GAMMA, gamma_at
            step(ts(lam[:, :], sc[:, 16:18, 0], -1.0, 1.0, ALU.mult, ALU.add))
            v.wait_ge(setup_a, 7)
            for k in range(KT):
                for c in range(2):
                    step(ts(cT[c][:, k, :], cT[c][:, k, :], sc[:, 6 + k, 0:1], 1.0 - 2.0 * c, ALU.mult, ALU.mult))
            step(v.tensor_copy(ident_bf[:, :], ident[:, :]))
            step(v.tensor_copy(ident_h[:, :], ident[:, :]))
            step(v.tensor_copy(upto_bf[:, :], upto[:, :]))
            step(v.tensor_copy(tokid[:, :], small[:, 2 * E:2 * E + T]))
            v.wait_ge(setup_t, 2)
            for k in range(KT):
                step(v.tensor_copy(wqkv[0][:, k, D:NQKV], work[0][:, k * P:(k + 1) * P]))
            for b in range(2):
                for k in range(KT):
                    step(ts(wqkv[b][:, k, :], wqkv[b][:, k, :], normw[:, b, k:k + 1], None, ALU.mult))
            step(ts(tern_scale[:, :], work[1][:, 0:D], 1.0 / D, 1e-5, ALU.mult, ALU.max))
            step(ts(tmp[2][:, 0, :], tern_scale[:, :], 0.5, None, ALU.mult))
            step(ts(tmp[2][:, 1, :], tern_scale[:, :], -0.5, None, ALU.mult))
            for k in range(KT):
                step(tt(tmp[1][:, k, :], tmp[0][:, k, :], tmp[2][:, 0, :], ALU.is_gt))
                step(tt(tmp[1][:, 2 + k, :], tmp[0][:, k, :], tmp[2][:, 1, :], ALU.is_lt))
            step(tt(ternT[:, :, :], tmp[1][:, 0:KT, :], tmp[1][:, KT:2 * KT, :], ALU.subtract))
            assert n_done[0] == N_SETUP_V, n_done

            def layernorm_stats(chain, src, stats, mv, after):
                for t in range(T):
                    chained(chain, v.bn_stats(stats[:, t, :], src[:, t, :]), wait=(t == T - 1))
                alone(v)
                for t in range(T):
                    last = v.bn_aggr(mv[:, t, :], stats[:, t, :])
                    if t < T - 1:
                        chain.inc(last)
                last.then_inc(after.sem, 1)

            def prepare_qk(s, kind, chain, tick):
                yield tick
                v.wait_ge(sq_ready[kind].sem, sq_ready[kind].at(s))
                if came(s, 2 - 2 * kind):
                    v.wait_ge(rn_ready[1 - kind].sem, rounds(s, kind))
                v.tensor_reduce(nrm[:, 0, :], rot[:, :, :].rearrange("p t (h d) -> p (t h) d", d=HD), AX.X,
                                ALU.add).then_inc(ss_ready[kind].sem, 1)
                pairs = qk[:, :, :].rearrange("p t (h d two) -> p t h d two", h=H + KVH, two=2)
                rt = [r[:, :, :].rearrange("p t (h d) -> p t h d", h=H + KVH) for r in ropetmp]
                for j in range(2):
                    table = rope[:, kind, j].unsqueeze(2).broadcast_to([P, T, H + KVH, HD // 2])
                    chained(chain, tt(rt[j], pairs[:, :, :, :, j], table, ALU.mult), wait=(j == 1))
                yield tick + 2
                v.wait_ge(ss_ready[kind].sem, ss_ready[kind].at(s))
                rv = rot[:, :, :].rearrange("p t (h two d) -> p t h two d", h=H + KVH, two=2)
                chained(chain, tt(rv[:, :, :, 0, :], rt[0], rt[1], ALU.subtract), wait=False)
                v.wait_ge(rope_pool[kind].sem, rope_pool[kind].at(s))
                chained(chain, tt(rv[:, :, :, 1, :], rt[2], rt[3], ALU.add))
                yield tick + 4
                v.wait_ge(rn_ready[kind].sem, rn_ready[kind].at(s))
                flat = rot[:, :, :].rearrange("p t (h d) -> p (t h) d", d=HD)
                tt(flat, flat, nrm[:, 1, :].unsqueeze(2).broadcast_to([P, T * (H + KVH), HD]), ALU.mult
                   ).then_inc(qn_ready[kind].sem, 1)
                yield tick + 8
                v.wait_ge(qn_ready[kind].sem, qn_ready[kind].at(s))
                v.wait_ge(hi_ready[kind].sem, hi_ready[kind].at(s))
                hv = rot[:, :, :].rearrange("p t (h d) -> p t h d", h=H + KVH)
                chained(chain, tt(qx[:, :, :, 32:48], hv[:, :, 0:H, :], qx[:, :, :, 0:16], ALU.subtract), wait=False)
                for c in range(2):
                    last = tt(kx[:, :, :, c, 16:32], hv[:, :, H:, :], kx[:, :, :, c, 0:16], ALU.subtract)
                    if c == 0:
                        chain.inc(last)
                last.then_inc(qkx_ready[kind].sem, 1)

            def take_qkT(s, kind, chain):
                for half in range(2):
                    name = f"k{kind}_{half}"
                    yield TICK[name] + 1
                    v.wait_ge(made(name), made_at(name, s))
                    if half == 0 and came(s):
                        v.wait_ge(pv_done.sem, pv_done.at(s - 1, kind, STEPS_A - LAG))
                    for c in range(2):
                        rows_ = slice(64 * c, 64 * c + 64)
                        dst = kT[kind][rows_, c, 2 * half:2 * half + 2].rearrange("p t g k -> p (t g k)").bitcast(F32)
                        last = v.tensor_copy(dst, bank(name)[rows_, :])
                        if c == 0:
                            chain.inc(last)
                    last.then_inc(taken(name), 1)
                for qr in range(4):
                    name = f"q{kind}_{qr}"
                    yield TICK[name] + 1
                    v.wait_ge(made(name), made_at(name, s))
                    dst = qT[kind][:, 2 * qr:2 * qr + 2, :].rearrange("p a t -> p (a t)").bitcast(F32)
                    v.tensor_copy(dst, bank(name)[:, :]).then_inc(taken(name), 1)

            def attend(s, kind):
                yield LOCAL_AT * kind
                va[kind].start(s)
                for g in range(KVH - 1):
                    yield LOCAL_AT * kind + STEP * (4 * g + 7) + 1
                    take_rows(s, kind, g, va[kind])

            def take_rows(s, kind, g, chain):
                name = f"r{kind}_{g}"
                v.wait_ge(made(name), made_at(name, s))
                w = bank(name)[:, :].rearrange("p (t j c) -> p t j c", t=T, j=GH)
                chained(chain, v.reciprocal(rden[g % 2][:, :, :], w[:, :, :, HD]))
                dst = attn[:, :, g * GH * HD:(g + 1) * GH * HD].rearrange("p t (j d) -> p t j d", j=GH)
                tt(dst, w[:, :, :, 0:HD], rden[g % 2][:, :, :].unsqueeze(3).broadcast_to([P, T, GH, HD]), ALU.mult
                   ).then_inc(taken(name), 1)

            def finish(s, b, kind, tick, chain):
                yield tick + 7
                take_rows(s, kind, KVH - 1, chain)
                yield TICK[f"a{kind}_0"] + 1
                for k in range(KT):
                    name = f"a{kind}_{k}"
                    v.wait_ge(made(name), made_at(name, s))
                    v.tensor_copy(attnT[:, k, :], bank(name)[:, :]).then_inc(taken(name), 1)
                for n in range(2):
                    name = f"o{kind}_{n}"
                    yield TICK[name] + 1
                    v.wait_ge(made(name), made_at(name, s))
                    tt(x2[b][:, 2 * n:2 * n + 2, :], bank(name)[:, :].rearrange("p (t d) -> p t d", t=2),
                       (x2 if kind else xn)[b][:, 2 * n:2 * n + 2, :], ALU.add).then_inc(taken(name), 1)

            def attend_global(s, b):
                yield from attend(s, 0)
                yield from finish(s, b, 0, LOCAL_AT, va[0])

            def attend_local(s, b):
                yield from attend(s, 1)

            def ending(s, b):
                yield 3
                ve.start(s)
                yield from finish(s, b, 1, 0, ve)

            def take_second(s, name, dst):
                v.wait_ge(made(name), made_at(name, s))
                v.tensor_copy(dst[:, 1, :], bank(name)[:, :]).then_inc(taken(name), 1)

            def quantize(s):
                for n in range(2):
                    name = f"had{n}"
                    yield TAKEN[name]
                    if n == 0:
                        vq.start(s)
                    v.wait_ge(made(name), made_at(name, s))
                    v.wait_ge(made("had1"), made_at("had1", s))
                    w = bank(name)
                    t0 = 2 * n
                    chained(vq, v.tensor_reduce(sc[:, AMAX, t0:t0 + 2], w[:, :].rearrange("p (t d) -> p t d", t=2), AX.X,
                                                ALU.max, apply_absolute_value=True))
                    chained(vq, ts(sc[:, QSC, t0:t0 + 2], sc[:, AMAX, t0:t0 + 2], 1e-5, 1.0 / 7, ALU.max, ALU.mult))
                    chained(vq, v.reciprocal(sc[:, QINV, t0:t0 + 2], sc[:, QSC, t0:t0 + 2]))
                    for j in range(2):
                        last = ts(rounded[:, t0 + j, :], w[:, j * D:(j + 1) * D], sc[:, QINV, t0 + j:t0 + j + 1], MAGIC,
                                  ALU.mult, ALU.add)
                        if j == 0:
                            vq.inc(last)
                    last.then_inc(taken(name), 1)
                yield 36
                v.wait_ge(taken("had1"), taken_at("had1", s))
                chained(vq, ts(rounded, rounded, MAGIC, 7.0, ALU.subtract, ALU.min))
                ts(q_int[:, :, :], rounded, -8.0, None, ALU.max).then_inc(q_int_ready.sem, 1)
                yield TICK["qT"] + 1
                v.wait_ge(made("qT"), made_at("qT", s))
                v.tensor_copy(q_intT[:, :, :].rearrange("p k t -> p (k t)").bitcast(F32), bank("qT")[:, :]
                              ).then_inc(taken("qT"), 1)

            def front(s, b):
                yield 11
                vf.start(s)
                v.wait_ge(x_loaded.sem, x_loaded.at(s))
                layernorm_stats(vf, x_in, stats[0], mv[0], var_ready)
                yield 14
                v.wait_ge(rstd_ready.sem, rstd_ready.at(s))
                chained(vf, tt(sc[:, M1], mv[0][:, :, 1], sc[:, RSTD], ALU.mult))
                tt(sc[:, M2], sc[:, M1], sc[:, RSTD], ALU.mult).then_inc(msq_ready.sem, 1)
                for t in range(T):
                    last = ts(xn[b][:, t, :], x_in[:, t, :], mv[0][:, t, 0:1], sc[:, RSTD, t:t + 1], ALU.subtract, ALU.mult)
                    if t < T - 1:
                        vf.inc(last)
                last.then_inc(xn_ready.sem, 1)
                yield TICK["xT1"] + 1
                take_second(s, "xT1", xT)
                yield from merged(prepare_qk(s, 0, vf, 33), quantize(s))
                yield from take_qkT(s, 0, vf)

            def gating(s, b):
                for n in range(2):
                    name = f"ffn{n}"
                    yield TICK[name] + 1
                    if n == 0:
                        vg.start(s)
                    v.wait_ge(made(name), made_at(name, s))
                    for j in range(2):
                        t = 2 * n + j
                        last = stt(tmp[0][:, t, :], bank(name)[:, j * D:(j + 1) * D], sc[:, QSC, t:t + 1],
                                   tern_scale[:, :], ALU.mult, ALU.mult)
                        if j == 0:
                            vg.inc(last)
                    last.then_inc(taken(name), 1)
                yield 17
                v.wait_ge(exp_y.sem, exp_y.at(s))
                ts(tmp[1][:, :, :], tmp[1][:, :, :], float(2.0 ** 60), None, ALU.min).then_inc(exp_y_capped.sem, 1)
                yield 20
                v.wait_ge(sig_ready.sem, sig_ready.at(s))
                chained(vg, tt(gate[b][:, :, :], tmp[0][:, :, :], tmp[1][:, :, :], ALU.mult))

            def between(s, b):
                yield TICK["yT1"] + 1
                vm.start(s)
                take_second(s, "yT1", xT)
                yield from prepare_qk(s, 1, vm, 12)
                yield from take_qkT(s, 1, vm)

            def back(s, b):
                yield 15
                vb.start(s)
                v.wait_ge(taken("o1_1"), taken_at("o1_1", s))
                v.wait_ge(again_loaded.sem, again_loaded.at(s))
                chained(vb, tt(gate[b][:, :, :], x2[b][:, :, :], gate[b][:, :, :], ALU.mult))
                tt(x1[:, :, :], gate[b][:, :, :], x1[:, :, :], ALU.add).then_inc(x1_ready.sem, 1)
                v.wait_ge(x1_ready.sem, x1_ready.at(s))
                layernorm_stats(vb, x1, stats[1], mv[1], var2_ready)
                yield 19
                v.wait_ge(rstd2_ready.sem, rstd2_ready.at(s))
                if came(s):
                    v.wait_ge(skip_ready.sem, skip_ready.at(s - 1))
                if scattered.was(s):
                    v.wait_ge(scattered.sem, scattered.before(s))
                for t in range(T):
                    last = ts(xn2[:, t, :], x1[:, t, :], mv[1][:, t, 0:1], sc[:, RSTD2, t:t + 1], ALU.subtract, ALU.mult)
                    if t < T - 1:
                        vb.inc(last)
                last.then_inc(xn2_ready.sem, 1)
                yield TICK["zT1"] + 1
                take_second(s, "zT1", zT)
                yield TICK["logit"] + 1
                v.wait_ge(made("logit"), made_at("logit", s))
                w = bank("logit")[:, 0:T * E].rearrange("p (t e) -> p t e", t=T)

                def over_e(x):
                    return x.unsqueeze(2).broadcast_to([P, T, E])

                def over_t(x):
                    return x.unsqueeze(1).broadcast_to([P, T, E])
                chained(vb, v.tensor_reduce(sc[:, MX], w, AX.X, ALU.max))
                chained(vb, tt(lg[:, 0], w, over_e(sc[:, MX]), ALU.is_equal), wait=False)
                tt(lg[:, 3], w, over_e(sc[:, MX]), ALU.subtract).then_inc(taken("logit"), 1)
                v.wait_ge(taken("logit"), taken_at("logit", s))
                chained(vb, tt(lg[:, 0], lg[:, 0], over_t(small[:, E:2 * E]), ALU.mult))
                chained(vb, v.tensor_reduce(sc[:, MX2], lg[:, 0], AX.X, ALU.max))
                chained(vb, tt(lg[:, 1], lg[:, 0], over_e(sc[:, MX2]), ALU.is_equal))
                v.tensor_copy(oh_bf[:, :, :], lg[:, 1]).then_inc(oh_ready.sem, 1)
                yield TICK["count"] + 1
                chained(vb, tt(lg[:, 2], lg[:, 1], over_t(small[:, 0:E]), ALU.mult))
                chained(vb, v.tensor_reduce(sc[:, EID], lg[:, 2], AX.X, ALU.add))
                v.wait_ge(logit_e.sem, logit_e.at(s))
                chained(vb, v.tensor_reduce(sc[:, SE], lg[:, 4], AX.X, ALU.add))
                chained(vb, v.reciprocal(sc[:, PM], sc[:, SE]))
                v.wait_ge(made("count"), made_at("count", s))
                w = bank("count")
                chained(vb, tt(lg[:, 2], w[:, 0:T * E].rearrange("p (t e) -> p t e", t=T), over_t(base[:, :]), ALU.add))
                tt(base[:, :], base[:, :], w[:, T * E:(T + 1) * E], ALU.add).then_inc(taken("count"), 1)
                chained(vb, tt(lg[:, 2], lg[:, 2], lg[:, 1], ALU.mult))
                chained(vb, v.tensor_reduce(sc[:, POS], lg[:, 2], AX.X, ALU.add))
                chained(vb, ts(sc[:, KEPT], sc[:, POS], float(CAP), None, ALU.is_le))
                chained(vb, stt(sc[:, FLAT], sc[:, EID], float(CAP), sc[:, POS], ALU.mult, ALU.add))
                chained(vb, stt(sc[:, DIFF], sc[:, FLAT], -1.0, tokid[:, :], ALU.add, ALU.subtract))
                chained(vb, tt(sc[:, DIFF], sc[:, DIFF], sc[:, KEPT], ALU.mult))
                if routes_stored.was(s):
                    v.wait_ge(routes_stored.sem, routes_stored.before(s))
                chained(vb, tt(idx[0][:, :], sc[:, DIFF], tokid[:, :], ALU.add))
                chained(vb, ts(tokid[:, :], tokid[:, :], float(S), None, ALU.add))
                chained(vb, ts(sc[:, NK], sc[:, KEPT], -1.0, 1.0, ALU.mult, ALU.add))
                chained(vb, tt(sc[:, PM], sc[:, PM], sc[:, KEPT], ALU.mult))
                tt(fac[0][:, :], sc[:, PM], sc[:, NK], ALU.add).then_inc(route_ready.sem, 1)
                for h in range(KT):
                    at = TICK[f"u{h}_0"] + 1
                    yield at
                    if h:
                        v.wait_ge(hid_ready.sem, hid_ready.at(s, h))
                    c_, s_ = cosT[:, h, :], sinT[:, h, :]
                    v.wait_ge(made(f"u{h}_0"), made_at(f"u{h}_0", s))
                    re = bank(f"u{h}_0")
                    chained(vb, tt(lru[0], re[:, :], c_, ALU.mult), wait=False)
                    tt(lru[1], re[:, :], s_, ALU.mult).then_inc(taken(f"u{h}_0"), 1)
                    v.wait_ge(made(f"u{h}_1"), made_at(f"u{h}_1", s))
                    im = bank(f"u{h}_1")
                    chained(vb, tt(lru[2], im[:, :], c_, ALU.mult), wait=False)
                    tt(lru[3], im[:, :], s_, ALU.mult).then_inc(taken(f"u{h}_1"), 1)
                    yield at + 2
                    v.wait_ge(taken(f"u{h}_1"), taken_at(f"u{h}_1", s))
                    chained(vb, tt(lru[0], lru[0], lru[3], ALU.add), wait=False)
                    chained(vb, tt(lru[2], lru[2], lru[1], ALU.subtract))
                    decay = lam[:, h:h + 1].broadcast_to([P, S])
                    chained(vb, v.tensor_tensor_scan(lru[4], decay, lru[0], 0.0, ALU.mult, ALU.add), wait=False)
                    yield at + 4
                    chained(vb, v.tensor_tensor_scan(lru[5], decay, lru[2], 0.0, ALU.mult, ALU.add))
                    yield at + 6
                    chained(vb, tt(lru[0], lru[4], c_, ALU.mult), wait=False)
                    chained(vb, tt(lru[1], lru[5], s_, ALU.mult), wait=False)
                    chained(vb, tt(lru[2], lru[4], s_, ALU.mult), wait=False)
                    tt(lru[3], lru[5], c_, ALU.mult).then_inc(lru_ready.sem, 1)
                for n in range(2):
                    yield TICK[f"out{n}"] + 1
                    v.wait_ge(skip_ready.sem, skip_ready.at(s))
                    name = f"out{n}"
                    v.wait_ge(made(name), made_at(name, s))
                    tt(s_out[:, 2 * n:2 * n + 2, :], bank(name)[:, :].rearrange("p (t d) -> p t d", t=2),
                       s_out[:, 2 * n:2 * n + 2, :], ALU.add).then_inc(taken(name), 1)
            pipeline(v, front, gating, attend_global, between, attend_local, ending, back)

            def take_rowsT(n, nb):
                v.wait_ge(rowsT_made.sem, rowsT_made.at(n, 2))
                v.tensor_copy(rowsT[nb][:, 1, :], work[1][:, :]).then_inc(rowsT_v.sem, 1)

            def expert(e, b):
                for j in range(STEPS):
                    n, nb = e * STEPS + j, (b * STEPS + j) % 2
                    if j == 0:
                        take_rowsT(n, nb)
                    for g in range(1, FT, 2):
                        v.wait_ge(hidden_made.sem, hidden_made.at(n, g + 1))
                        if g == 1:
                            if down_made.was(n):
                                v.wait_ge(down_made.sem, down_made.before(n))
                        ts(hidden[:, g, :], ring[g % 4][:, :], 0.0, None, ALU.max).then_inc(relu_v.sem, 1)
                    if j < STEPS - 1:
                        take_rowsT(n + 1, 1 - nb)
            experts(v, expert)

            def last_part(s, b):
                v_end.start(s)
                v.wait_ge(g_loaded.sems[b], g_loaded.at(s, b))
                v.wait_ge(g_gathered.sems[b], g_gathered.at(s, b))
                for t in range(T):
                    last = ts(tmp[0][:, t, :], end_g[b][:, t, :], fac[b][:, t:t + 1], None, ALU.mult)
                    if t < T - 1:
                        v_end.inc(last)
                last.then_inc(z_ready.sem, 1)
                v.wait_ge(z_exp.sem, z_exp.at(s))
                ts(tmp[1][:, :, :], tmp[1][:, :, :], float(2.0 ** 60), None, ALU.min).then_inc(z_capped.sem, 1)
                v_end.inc(tt(end_tmp, tmp[0][:, :, :], end_s[b][:, :, :], ALU.mult))
                v.wait_ge(z_sig.sem, z_sig.at(s))
                v.wait_ge(v_end.sem, v_end.at())
                v_end.inc(tt(end_tmp, end_tmp, tmp[1][:, :, :], ALU.mult))
                v.wait_ge(v_end.sem, v_end.at())
                if came(s, 2):
                    v.wait_ge(out_stored.sems[b], out_stored.at(s - 2, b))
                tt(end_out[b][:, :, :], end_tmp, end_x1[b][:, :, :], ALU.add).then_inc(out_ready.sem, 1)
            sequences(v, last_part)


_ARGS = {
    "x": ("L0_attn_hidden", lambda v: v.reshape(NTOK, D)),
    "norm1T": ("L0_attn_norm1_w", lambda v: v.reshape(KT, P).T),
    "norm2T": ("L0_attn_norm2_w", lambda v: v.reshape(KT, P).T),
    "downT": ("L0_attn_g_kv_down", lambda v: v.T),
    "ffn_wT": ("L0_ffn_weight", lambda v: v.T),
    "B_reT": ("L1_attn_B_re", lambda v: v.T),
    "B_imT": ("L1_attn_B_im", lambda v: v.T),
    "C_reT": ("L1_attn_C_re", lambda v: v.T),
    "C_imT": ("L1_attn_C_im", lambda v: v.T),
    "D_skip": ("L1_attn_D_skip", lambda v: v),
    "W1": ("L1_ffn_W1", lambda v: v),
    "W2": ("L1_ffn_W2", lambda v: v),
}
_PLAIN = ["L0_attn_g_wq", "L0_attn_g_k_up", "L0_attn_g_v_up", "L0_attn_g_wo", "L0_attn_l_wq", "L0_attn_l_wk",
          "L0_attn_l_wv", "L0_attn_l_wo", "L1_ffn_Wr"]


def kernel(**inputs):
    import concourse.bacc as bacc
    from concourse.bass_utils import run_bass_kernel_spmd

    host = {n: lay(np.asarray(inputs[src])) for n, (src, lay) in _ARGS.items()}
    host.update({n: np.asarray(inputs[n]) for n in _PLAIN})
    host["lru_logs"] = np.concatenate([np.asarray(inputs[n]).reshape(KT, P).T for n in ("L1_attn_nu_log", "L1_attn_theta_log")], axis=1)
    host.update(shape_constants())
    nc = bacc.Bacc("TRN2", target_bir_lowering=False, num_devices=1)
    arrays, aps = {}, {}
    for name, value in host.items():
        value = np.ascontiguousarray(value)
        arrays[f"in_{name}"] = value
        aps[name] = nc.dram_tensor(f"in_{name}", value.shape, mybir.dt.from_np(value.dtype), kind="ExternalInput").ap()
    out = nc.dram_tensor("out", [NTOK, D], F32, kind="ExternalOutput").ap()
    build_program(nc, aps, out)
    r = run_bass_kernel_spmd(nc, [arrays], core_ids=[0])
    return np.asarray(r.results[0]["out"]).reshape(NSEQ, S, D)
```
